# Optimizing a Trainium2 kernel written in Bass

```python
import numpy as np
import jax
import jax.numpy as jnp

def _softmax(x, axis=-1):
    return jax.nn.softmax(x, axis=axis)

def _gelu(x):
    return jax.nn.gelu(x, approximate=True)

def _silu(x):
    return jax.nn.silu(x)

def _sigmoid(x):
    return jax.nn.sigmoid(x)

def _layernorm(x, axis=-1, eps=1e-05):
    m = jnp.mean(x, axis=axis, keepdims=True)
    v = jnp.var(x, axis=axis, keepdims=True)
    return (x - m) / jnp.sqrt(v + eps)

def _scatter_add(tgt, idx, src, axis=0):
    return tgt.at[idx].add(src)

def _segment_sum(src, seg, n):
    return jax.ops.segment_sum(src, seg, n)
kernel_name = 'mk_adj_ffn_d1_adj_r2_09ede4'

def setup_inputs(seed: int=0):
    np.random.seed(seed)
    _w = jnp.asarray

    def _rec_inputs():
        import jax
        import jax.numpy as jnp
        _gk = jax.random.key(seed)
        x = -0.0005207 + 1.001 * jax.random.normal(jax.random.fold_in(_gk, 1), (64, 128, 128), jnp.float32)
        _w = (1.0 + jnp.arange(128, dtype=jnp.float32)) ** (-0.5)
        _w = _w / _w.mean()
        _pij = jnp.clip(0.03125 * _w[:, None] * _w[None, :], 0.0, 1.0)
        _a = jax.random.uniform(jax.random.fold_in(_gk, 2), (64, 128, 128)) < _pij
        _a = jnp.logical_or(_a, jnp.swapaxes(_a, -1, -2))
        _a = jnp.logical_or(_a, jnp.eye(128, dtype=bool))
        _af = _a.astype(jnp.float32)
        _af = _af * jax.random.uniform(jax.random.fold_in(_gk, 3), (64, 128, 128), jnp.float32, 0.05, 1)
        adj = _af
        return (x, adj)
    x, adj = _rec_inputs()

    def _L0_gnn_setup():
        import jax, jax.numpy as jnp
        import numpy as np
        H = 4
        LN_EPS = 1e-05

        def _heads(x, B, N):
            return x.reshape(B, N, H, -1).transpose(0, 2, 1, 3)
        key = jax.random.key(seed)
        ks = jax.random.split(key, 6)
        B, N, IN, OUT = (4, 1024, 128, 128)
        return {'node_feats': jax.random.normal(ks[0], (B, N, IN), dtype=jnp.float32), 'adj_matrix': jax.random.uniform(ks[1], (B, N, N), dtype=jnp.float32), 'W_lin': jax.random.normal(ks[2], (IN, OUT), dtype=jnp.float32) * IN ** (-0.5), 'b_lin': jnp.zeros((OUT,), dtype=jnp.float32), 'W_q': jax.random.normal(ks[3], (IN, OUT), dtype=jnp.float32) * IN ** (-0.5), 'W_k': jax.random.normal(ks[4], (IN, OUT), dtype=jnp.float32) * IN ** (-0.5), 'ln_g': jnp.ones((OUT,), dtype=jnp.float32), 'ln_b': jnp.zeros((OUT,), dtype=jnp.float32)}
    _L0_gnn_all = _L0_gnn_setup()
    _L0_gnn_in = {k: v for k, v in _L0_gnn_all.items() if k in ('W_lin', 'b_lin', 'W_q', 'W_k', 'ln_g', 'ln_b')}
    del _L0_gnn_all

    def _L0_ffn_setup():
        import jax, jax.numpy as jnp
        import numpy as np
        B, T, D, H, E = (16, 2048, 128, 256, 8)
        key = jax.random.key(seed)
        ks = jax.random.split(key, 5)
        x = jax.random.normal(ks[0], (B, T, D), dtype=jnp.float32)
        gate_w = jax.random.normal(ks[1], (D, E), dtype=jnp.float32) * 0.02
        gate_b = jnp.zeros((E,), dtype=jnp.float32)
        W1 = jax.random.normal(ks[2], (E, D, H), dtype=jnp.float32) * 0.02
        b1 = jnp.zeros((E, H), dtype=jnp.float32)
        W2 = jax.random.normal(ks[3], (E, H, D), dtype=jnp.float32) * 0.02
        b2 = jnp.zeros((E, D), dtype=jnp.float32)
        return {'x': x, 'gate_w': gate_w, 'gate_b': gate_b, 'W1': W1, 'b1': b1, 'W2': W2, 'b2': b2}
    _L0_ffn_all = _L0_ffn_setup()
    _L0_ffn_in = {k: v for k, v in _L0_ffn_all.items() if k in ('gate_w', 'gate_b', 'W1', 'b1', 'W2', 'b2')}
    del _L0_ffn_all
    return {'x': x, 'adj': adj, 'L0_gnn_W_lin': _L0_gnn_in['W_lin'], 'L0_gnn_b_lin': _L0_gnn_in['b_lin'], 'L0_gnn_W_q': _L0_gnn_in['W_q'], 'L0_gnn_W_k': _L0_gnn_in['W_k'], 'L0_gnn_ln_g': _L0_gnn_in['ln_g'], 'L0_gnn_ln_b': _L0_gnn_in['ln_b'], 'L0_ffn_gate_w': _L0_ffn_in['gate_w'], 'L0_ffn_gate_b': _L0_ffn_in['gate_b'], 'L0_ffn_W1': _L0_ffn_in['W1'], 'L0_ffn_b1': _L0_ffn_in['b1'], 'L0_ffn_W2': _L0_ffn_in['W2'], 'L0_ffn_b2': _L0_ffn_in['b2']}

def reference(x, adj, L0_gnn_W_lin, L0_gnn_b_lin, L0_gnn_W_q, L0_gnn_W_k, L0_gnn_ln_g, L0_gnn_ln_b, L0_ffn_gate_w, L0_ffn_gate_b, L0_ffn_W1, L0_ffn_b1, L0_ffn_W2, L0_ffn_b2):
    import jax
    import jax.numpy as jnp

    def _L0_gnn_ref(node_feats, adj_matrix, W_lin, b_lin, W_q, W_k, ln_g, ln_b):
        import jax, jax.numpy as jnp
        import numpy as np
        H = 4
        LN_EPS = 1e-05

        def _heads(x, B, N):
            return x.reshape(B, N, H, -1).transpose(0, 2, 1, 3)
        B, N, _ = node_feats.shape
        out_dim = W_lin.shape[1]
        hd = out_dim // H
        scale = hd ** (-0.5)
        lrelu = lambda z: jax.nn.leaky_relu(z, 0.01)
        X = _heads(lrelu(node_feats @ W_lin + b_lin), B, N)
        q = _heads(lrelu(node_feats @ W_q), B, N)
        k = _heads(lrelu(node_feats @ W_k), B, N)
        att = jax.nn.sigmoid(jnp.einsum('bhxd,bhyd->bhxy', q, k) * scale)
        adj_h = adj_matrix[:, None] * att
        deg = jnp.sum(adj_h, axis=-1)
        dis = jnp.where(deg > 0, deg ** (-0.5), 0.0)
        A = dis[..., :, None] * adj_h * dis[..., None, :]
        Y = jnp.einsum('bhxy,bhyd->bhxd', A, X)
        Y = Y.transpose(0, 2, 1, 3).reshape(B, N, out_dim)
        mu = jnp.mean(Y, axis=-1, keepdims=True)
        var = jnp.mean((Y - mu) ** 2, axis=-1, keepdims=True)
        return (Y - mu) * jax.lax.rsqrt(var + LN_EPS) * ln_g + ln_b

    def _L0_ffn_ref(x, gate_w, gate_b, W1, b1, W2, b2):
        import jax, jax.numpy as jnp
        import numpy as np
        B, T, D, H, E = (16, 2048, 128, 256, 8)
        Bb, Tt, Dd = x.shape
        Ee = gate_w.shape[1]
        xf = x.reshape(-1, Dd)
        N = xf.shape[0]
        logits = xf @ gate_w + gate_b
        probs = jax.nn.softmax(logits, axis=-1)
        top2_vals, top2_idx = jax.lax.top_k(probs, 2)
        cw = jnp.zeros((N, Ee), dtype=xf.dtype).at[jnp.arange(N)[:, None], top2_idx].add(top2_vals)

        def step(acc, params):
            w1, bb1, w2, bb2, we = params
            h = jax.nn.gelu(xf @ w1 + bb1, approximate=False)
            y = h @ w2 + bb2
            return (acc + we[:, None] * y, None)
        out, _ = jax.lax.scan(step, jnp.zeros_like(xf), (W1, b1, W2, b2, cw.T))
        return out.reshape(Bb, Tt, Dd)
    x = x + _L0_gnn_ref(_layernorm(x, axis=-1), adj, L0_gnn_W_lin, L0_gnn_b_lin, L0_gnn_W_q, L0_gnn_W_k, L0_gnn_ln_g, L0_gnn_ln_b)
    x = x + _L0_ffn_ref(_layernorm(x, axis=-1), L0_ffn_gate_w, L0_ffn_gate_b, L0_ffn_W1, L0_ffn_b1, L0_ffn_W2, L0_ffn_b2)
    return x

_drawn_inputs = setup_inputs


def setup_inputs(seed=0):
    import zlib

    import numpy as np

    out = dict(_drawn_inputs(seed))
    spreads = {'L0_gnn_b_lin': (0.0, 0.1),
     'L0_gnn_ln_g': (1.0, 0.2),
     'L0_gnn_ln_b': (0.0, 0.1),
     'L0_ffn_gate_b': (0.0, 0.681),
     'L0_ffn_b1': (0.0, 0.8),
     'L0_ffn_b2': (0.0, 0.512)}
    factors = {'L0_ffn_gate_w': 3.896, 'L0_ffn_W1': 8.0, 'L0_ffn_W2': 8.0}
    for name, (base, spread) in spreads.items():
        noise = np.random.default_rng([zlib.crc32(name.encode()), seed]).standard_normal(out[name].shape)
        drawn = base * np.exp(spread * noise) if base else spread * noise
        out[name] = jnp.asarray(drawn.astype(out[name].dtype))
    for name, factor in factors.items():
        out[name] = (out[name] * factor).astype(out[name].dtype)
    return out
```

```python
import concourse.bass as bass
from concourse import mybir
from contextlib import ExitStack


def graph_block_kernel(
    nc: bass.Bass,
    x: bass.AP,
    adj: bass.AP,
    w_lin: bass.AP,
    b_lin: bass.AP,
    w_q: bass.AP,
    w_k: bass.AP,
    ln_g: bass.AP,
    ln_b: bass.AP,
    gate_w: bass.AP,
    gate_b: bass.AP,
    w1: bass.AP,
    b1: bass.AP,
    w2: bass.AP,
    b2: bass.AP,
    out: bass.AP,
):
    f32 = mybir.dt.float32
    f32r = mybir.dt.float32r
    bf16 = mybir.dt.bfloat16
    i32 = mybir.dt.int32
    u32 = mybir.dt.uint32
    ALU = mybir.AluOpType
    ACT = mybir.ActivationFunctionType
    AX = mybir.AxisListType
    ds = bass.ds

    P = 128
    GRAPHS, N, D = x.shape
    E = gate_w.shape[1]
    HID = w1.shape[2]
    H = 4
    HD = D // H
    SCALE = float(HD) ** -0.5
    LEAK = 0.01
    EPS = 1e-5
    TINY = 1.2e-38
    G = 2
    PAIRS = GRAPHS // G
    GD = G * D
    GH = G * H
    NODES = GRAPHS * N

    NP = E * (E - 1) // 2
    REGION = NODES + P
    DUMMY_ROW = NP * REGION
    TILES = (NODES + NP * (P - 1)) // P
    KC = HID // P
    ROW = D + 8
    C_WA, C_WB, C_MEAN, C_RSTD, C_NODE = D, D + 1, D + 2, D + 3, D + 4
    NO_NODE = 1 << 20

    x_t = x.rearrange("g n d -> n g d")
    adj_t = adj.rearrange("g n m -> n g m")
    out_rows = out.rearrange("g n d -> (g n) d")
    slots = nc.dram_tensor("slots", (DUMMY_ROW + P, ROW), f32).ap()

    ctx = ExitStack()
    with ctx:
        def sb(name, shape, dt=f32):
            return ctx.enter_context(nc.sbuf_tensor(name, shape, dt))

        def pb(name, shape, dt=f32):
            return ctx.enter_context(nc.psum_tensor(name, shape, dt))

        def sem(name):
            return ctx.enter_context(nc.semaphore(name))

        ident = sb("ident", [P, P])
        before = sb("before", [P, P], bf16)
        ones = sb("ones", [P, P], bf16)
        pair_no = sb("pair_no", [P, NP])
        pair_start = sb("pair_start", [P, NP])
        node_no = sb("node_no", [P, GRAPHS], i32)
        tri = sb("tri", [P, E - 1])
        part_no = sb("part_no", [P, 1])
        neg_half = sb("neg_half", [P, GH])
        eps_t = sb("eps_t", [P, G])
        wlin_sb = sb("wlin_sb", [D, D])
        wq_sb = sb("wq_sb", [D, D])
        wk_sb = sb("wk_sb", [D, D])
        gatew_sb = sb("gatew_sb", [D, E])
        blin_bc = sb("blin_bc", [P, D])
        lng_bc = sb("lng_bc", [P, D])
        lnb_bc = sb("lnb_bc", [P, D])
        gateb_bc = sb("gateb_bc", [P, E])
        w1_sb = sb("w1_sb", [D, E * HID])
        w1_hi = sb("w1_hi", [D, E * HID], f32r)
        w1_lo = sb("w1_lo", [D, E * HID], f32r)
        w2_sb = sb("w2_sb", [P, E * KC, D])
        b1_bc = sb("b1_bc", [P, E * HID])
        b2_bc = sb("b2_bc", [P, E * D])
        filler = sb("filler", [P, ROW])

        xin = sb("xin", [P, 4, G, D])
        adjin = sb("adjin", [P, 4, G, N])
        st1 = sb("st1", [P, 2, G, 6])
        mv1 = sb("mv1", [P, 2, G, 2])
        ve1 = sb("ve1", [P, 2, G])
        rs1 = sb("rs1", [P, 2, G])
        nrm = sb("nrm", [P, 2, G, D])
        nrmT = sb("nrmT", [D, 2, G, N])
        qbd = sb("qbd", [D, 2, G, H, N])
        qkc = sb("qkc", [D, 2, 2, G, N])
        qkl = sb("qkl", [D, 2, 2, G, N])
        xlb = sb("xlb", [P, 2, G, D])
        xl = sb("xl", [P, 2, G, D])
        att = sb("att", [P, 2, G, H, N])
        adjh = sb("adjh", [P, 2, G, H, N])
        deg = sb("deg", [P, 2, GH])
        degm = sb("degm", [P, 2, GH])
        degc = sb("degc", [P, 2, GH])
        degp = sb("degp", [P, 2, GH])
        dis = sb("dis", [P, 4, GH])
        adjhT = sb("adjhT", [P, 2, G, H, N])
        xs = sb("xs", [P, 2, G, D])
        yT = sb("yT", [D, 2, G, N])
        yv = sb("yv", [P, 2, G, D])
        st2 = sb("st2", [P, 2, G, 6])
        mv2 = sb("mv2", [P, 2, G, 2])
        ve2 = sb("ve2", [P, 2, G])
        rs2 = sb("rs2", [P, 2, G])
        yn = sb("yn", [P, 2, G, D])
        yg = sb("yg", [P, 2, G, D])
        xb = sb("xb", [P, 2, G, D])
        rows = sb("rows", [P, 4, G, ROW])
        st3 = sb("st3", [P, 2, G, 6])
        mv3 = sb("mv3", [P, 2, G, 2])
        ve3 = sb("ve3", [P, 2, G])
        rs3 = sb("rs3", [P, 2, G])
        n3 = sb("n3", [P, 2, G, D])
        n3T = sb("n3T", [D, 2, G, N])
        lg = sb("lg", [P, 2, G, E])
        mx = sb("mx", [P, 2, G, E])
        ix = sb("ix", [P, 2, G, E], u32)
        zz = sb("zz", [P, 2, G, E])
        sp = sb("sp", [P, 2, G, E])
        sn = sb("sn", [P, 2, G, E])
        rn = sb("rn", [P, 2, G, E])
        ez = sb("ez", [P, 2, G, E])
        es = sb("es", [P, 2, G])
        er = sb("er", [P, 2, G])
        w12 = sb("w12", [P, 2, G, 2])
        ixf = sb("ixf", [P, 2, G, 2])
        ea = sb("ea", [P, 2, G])
        eb = sb("eb", [P, 2, G])
        tb = sb("tb", [P, 2, G])
        pid = sb("pid", [P, 2, G])
        sel = sb("sel", [P, 2, G])
        dw = sb("dw", [P, 2, G])
        sdw = sb("sdw", [P, 2, G])
        sw = sb("sw", [P, 2, G])
        oh = sb("oh", [P, 2, G, NP], bf16)
        seen = sb("seen", [P, 4, NP], bf16)
        seen1 = sb("seen1", [P, 2, NP], bf16)
        slot_t = sb("slot_t", [P, 2, NP])
        pos = sb("pos", [P, 2, G])
        base = sb("base", [P, 2, G])
        slot = sb("slot", [P, 4, G], u32)

        cnt = sb("cnt", [P, NP])
        cnti = sb("cnti", [P, NP], i32)
        tilesi = sb("tilesi", [P, NP], i32)
        tilesf = sb("tilesf", [P, NP])
        zero28 = sb("zero28", [P, NP])
        cum = sb("cum", [P, NP])
        past = sb("past", [P, NP])
        scr28 = sb("scr28", [P, NP])
        ge7 = sb("ge7", [P, E - 1])
        scr7 = sb("scr7", [P, E - 1])
        tinfo = sb("tinfo", [P, 8])
        padrow = sb("padrow", [P, NP], i32)
        desc = sb("desc", [1, 3 * P], i32)
        R2 = 4
        rin = sb("rin", [P, R2, ROW])
        rid = sb("rid", [P, R2], u32)
        nx = sb("nx", [P, R2, D])
        xh = sb("xh", [D, R2, P], f32r)
        xo = sb("xo", [D, R2, P], f32r)
        hb = sb("hb", [P, R2, 2 * HID])
        hg = sb("hg", [P, R2, 2 * HID])
        hT = sb("hT", [P, R2, 2 * KC, P])
        ra = sb("ra", [P, R2, D])
        rb = sb("rb", [P, R2, D])
        rc = sb("rc", [P, R2, D])
        ro = sb("ro", [P, R2, D])

        bank = [pb(f"bank{i}", [P, 512]) for i in range(8)]
        pS = [bank[0], bank[1]]
        pE = [bank[2], bank[3]]
        pQK = bank[4]
        pX = bank[5]
        pYT = bank[6]
        pY = bank[7]

        s_const = sem("s_const")
        s_iota_c = sem("s_iota_c")
        s_chain = sem("s_chain")
        s_passed = {e: sem(f"s_passed_{n}") for n, e in (("dve", nc.vector.engine), ("pool", nc.gpsimd.engine))}
        s_iota = sem("s_iota")
        s_par = sem("s_par")
        s_w1 = sem("s_w1")
        s_w1hi = sem("s_w1hi")
        s_w1lo = sem("s_w1lo")
        s_x = [sem(f"s_x{r}") for r in range(4)]
        s_adj = [sem(f"s_adj{r}") for r in range(4)]
        names = ("st1 mv1 ve1 rs1 nrm nTp nrmT qk Xp qkc qkl qT xlb xl S att adjh degc degm degp dis "
                 "Ep adjhT xs YTp yT Yp yv st2 mv2 ve2 rs2 yn yg xb res st3 mv3 ve3 rs3 n3 n3Tp n3T "
                 "Lp lg mx ix zz sp sn rn ez es er w12 ixf ea eb tb pid sel dw sdw sw wa row "
                 "oh seen seen1 rank slott pos base slot").split()
        S = {n: sem("p_" + n) for n in names}
        s_scat = [sem(f"s_scat{r}") for r in range(4)]
        names2 = "nx T1 xh xo L1 hb hg Tg hT L2 ra rb rc ro rid".split()
        Q = {n: sem("q_" + n) for n in names2}
        q_in = [sem(f"q_in{r}") for r in range(R2)]
        q_out = [sem(f"q_out{r}") for r in range(R2)]
        s_cnt = sem("s_cnt")
        s_plan = sem("s_plan")
        s_tin = sem("s_tin")
        s_descp = sem("s_descp")
        s_desc = sem("s_desc")
        s_pad = sem("s_pad")

        block = ctx.enter_context(nc.Block())

        def reached(eng, s, v):
            if isinstance(v, int) and v <= 0:
                return
            eng.wait_ge(s, v)

        def reached_alone(eng, s, v):
            if isinstance(v, int):
                return reached(eng, s, v)
            eng.wait_ge(s, v)
            eng.sem_inc(s_passed[eng.engine], 1)

        STEPS = PAIRS + 4
        FIRST, BODY = 8, 4
        LOOPED = (PAIRS - 1 - FIRST) // BODY * BODY

        def pipeline(eng, step):
            for i in range(FIRST):
                step(i, i)
            with eng.Fori(0, LOOPED // BODY) as turn:
                for k in range(BODY):
                    step(turn * BODY + (FIRST + k), FIRST + k)
            for i in range(FIRST + LOOPED, STEPS):
                step(i, i)

        def live(k, lag):
            return 0 <= k - lag < PAIRS

        WEIGHTS_AT, HI_AT, LO_AT = 2, 6, 7

        T_FIRST = 8
        T_LOOPED = (TILES - T_FIRST) // R2 * R2

        def tiles(eng, step):
            for t in range(T_FIRST):
                step(t, t)
            with eng.Fori(0, T_LOOPED // R2) as turn:
                for k in range(R2):
                    step(turn * R2 + (T_FIRST + k), T_FIRST + k)
            for t in range(T_FIRST + T_LOOPED, TILES):
                step(t, t)

        def ring_count(i, k, per):
            q = k % 4
            if isinstance(i, int):
                return per * ((i - q) // 4 + 1)
            return (i - q) * (per // 4) + per

        def tiles_skewed(eng, step):
            for t in range(T_FIRST):
                step(t, t)
            with eng.Fori(0, T_LOOPED // R2 - 1) as turn:
                for k in range(R2):
                    step(turn * R2 + (T_FIRST + k), T_FIRST + k)
            for t in range(T_FIRST + T_LOOPED - R2, TILES + 2):
                step(t, t)

        @block.sync
        def _(sp_):
            for dst, src in ((wq_sb, w_q), (wk_sb, w_k), (wlin_sb, w_lin), (gatew_sb, gate_w)):
                sp_.dma_start(dst[:, :], src).then_inc(s_par, 16)
            for dst, src in ((blin_bc, b_lin), (lng_bc, ln_g), (lnb_bc, ln_b), (gateb_bc, gate_b)):
                sp_.dma_start(dst[:, :], src.partition_broadcast(P)).then_inc(s_par, 16)

            def step(i, k):
                if isinstance(i, int) and i == WEIGHTS_AT:
                    sp_.dma_start(w1_sb[:, :].rearrange("p (e h) -> p e h", e=E), w1.rearrange("e p h -> p e h")).then_inc(s_w1, 16)
                    sp_.dma_start(w2_sb[:, :, :], w2.rearrange("e (c p) d -> p (e c) d", p=P)).then_inc(s_w1, 16)
                    sp_.dma_start(b1_bc[:, :], b1.rearrange("e h -> (e h)").partition_broadcast(P)).then_inc(s_w1, 16)
                    sp_.dma_start(b2_bc[:, :], b2.rearrange("e d -> (e d)").partition_broadcast(P)).then_inc(s_w1, 16)
                if k + 2 >= PAIRS:
                    return
                r = (k + 2) % 4
                reached(sp_, S["xb"], (i - 1) if k - 1 > 0 else 0)
                reached(sp_, S["adjh"], (i - 1) if k - 1 > 0 else 0)
                sp_.dma_start(xin[:, r, :, :], x_t[:, ds((i + 2) * G, G), :]).then_inc(s_x[r], 16)
                sp_.dma_start(adjin[:, r, :, :], adj_t[:, ds((i + 2) * G, G), :]).then_inc(s_adj[r], 16)

            for p in range(2):
                sp_.dma_start(xin[:, p, :, :], x_t[:, p * G:(p + 1) * G, :]).then_inc(s_x[p], 16)
                sp_.dma_start(adjin[:, p, :, :], adj_t[:, p * G:(p + 1) * G, :]).then_inc(s_adj[p], 16)
            pipeline(sp_, step)

            sp_.wait_ge(s_plan, 1)
            for p in range(NP):
                row = sp_.value_load(padrow[0:1, p:p + 1], min_val=0, max_val=DUMMY_ROW)
                sp_.dma_start(slots[ds(row, P), :], filler[:, :]).then_inc(s_pad, 16)
            sp_.dma_start(slots[DUMMY_ROW:DUMMY_ROW + P, :], filler[:, :]).then_inc(s_pad, 16)
            sp_.wait_ge(s_pad, 16 * (NP + 1))
            for r in range(4):
                sp_.wait_ge(s_scat[r], 16 * G * (PAIRS // 4))
            sp_.wait_ge(s_desc, 1)

            def load_tile(t, k):
                r = k % R2
                reached(sp_, Q["ro"], (t - R2 + 1) if k >= R2 else 0)
                row = sp_.value_load(desc[0:1, ds(t, 1)], min_val=0, max_val=DUMMY_ROW)
                sp_.dma_start(rin[:, r, :], slots[ds(row, P), :]).then_inc(q_in[r], 16)
            tiles(sp_, load_tile)

        @block.tensor
        def _(pe):
            mm = nc.tensor.matmul
            pe.wait_ge(s_const, 1)
            pe.wait_ge(s_iota, 1)
            pe.wait_ge(s_par, 16 * 8)

            def norm_T(i, k):
                b = k % 2
                reached(pe, S["nrm"], i + 1)
                reached(pe, S["qkc"], i)
                for g in range(G):
                    last = nc.tensor.transpose(pQK[:, g * N:(g + 1) * N], nrm[:, b, g, :], ident[:, :])
                last.then_inc(S["nTp"], 1)

            def step(i, k):
                if k == 0:
                    norm_T(0, 0)
                if live(k, 0):
                    b = k % 2
                    reached(pe, S["nrmT"], i + 1)
                    mm(pQK[:, 0:GD], wq_sb[:, :], nrmT[:, b, :, :].rearrange("p g n -> p (g n)"), start=True, stop=True)
                    mm(pQK[:, GD:2 * GD], wk_sb[:, :], nrmT[:, b, :, :].rearrange("p g n -> p (g n)"), start=True, stop=True).then_inc(S["qk"], 1)
                    if k >= 1:
                        reached(pe, S["xlb"], i)
                    if live(k, 3):
                        reached(pe, S["n3T"], i - 2)
                    for g in range(G):
                        last = mm(pX[:, g * D:(g + 1) * D], nrmT[:, b, g, :], wlin_sb[:, :], start=True, stop=True)
                    last.then_inc(S["Xp"], 1)
                if live(k, 1):
                    b = (k - 1) % 2
                    reached(pe, S["adjh"], i)
                    if k >= 2:
                        reached(pe, S["adjhT"], i - 1)
                    for g in range(G):
                        for h in range(H):
                            last = nc.tensor.transpose(pE[g][:, h * N:(h + 1) * N], adjh[:, b, g, h, :], ident[:, :])
                    last.then_inc(S["Ep"], 1)
                if live(k, 3):
                    b = (k - 3) % 2
                    reached(pe, S["oh"], i - 2)
                    reached(pe, S["seen"], i - 2)
                    reached(pe, S["yv"], min(i - 1, PAIRS) if isinstance(i, int) else i - 1)
                    for g in range(G):
                        o = pY[:, GD + g * NP:GD + (g + 1) * NP]
                        mm(o, before[:, :], oh[:, b, g, :], start=True, stop=False)
                        prior = seen[:, (k - 3) % 4, :] if g == 0 else seen1[:, b, :]
                        last = mm(o, ones[:, :], prior, start=False, stop=True)
                    last.then_inc(S["rank"], 1)
                if live(k, 0):
                    b = k % 2
                    reached(pe, S["qT"], i + 1)
                    if k >= 1:
                        reached(pe, S["att"], i)
                    for g in range(G):
                        for h in range(H):
                            last = mm(pS[g][:, h * N:(h + 1) * N], qbd[:, b, g, h, :], qkl[:, b, 1, g, :], start=True, stop=True)
                    last.then_inc(S["S"], 1)
                if live(k, 1):
                    b = (k - 1) % 2
                    reached(pe, S["adjhT"], i)
                    reached(pe, S["xs"], i)
                    if k >= 2:
                        reached(pe, S["yT"], i - 1)
                    if live(k, 3):
                        reached(pe, S["lg"], i - 2)
                    for g in range(G):
                        for h in range(H):
                            last = mm(pYT[h * HD:(h + 1) * HD, g * N:(g + 1) * N], xs[:, b, g, h * HD:(h + 1) * HD],
                                      adjhT[:, b, g, h, :], start=True, stop=True, skip_group_check=True)
                    last.then_inc(S["YTp"], 1)
                if live(k + 1, 0):
                    norm_T(i + 1, k + 1)
                if live(k, 2):
                    b = (k - 2) % 2
                    reached(pe, S["n3"], i - 1)
                    if live(k, 0):
                        reached(pe, S["xlb"], i + 1)
                    for g in range(G):
                        last = nc.tensor.transpose(pX[:, g * N:(g + 1) * N], n3[:, b, g, :], ident[:, :])
                    last.then_inc(S["n3Tp"], 1)
                if live(k, 1):
                    b = (k - 1) % 2
                    reached(pe, S["yT"], i)
                    if k >= 2:
                        reached(pe, S["yv"], i - 1)
                    if live(k, 3):
                        reached(pe, S["slott"], i - 2)
                    for g in range(G):
                        last = nc.tensor.transpose(pY[:, g * D:(g + 1) * D], yT[:, b, g, :], ident[:, :])
                    last.then_inc(S["Yp"], 1)
                if live(k, 2):
                    b = (k - 2) % 2
                    reached(pe, S["n3T"], i - 1)
                    if live(k, 1):
                        reached(pe, S["yT"], i)
                    if live(k, 3):
                        reached(pe, S["lg"], i - 2)
                    for g in range(G):
                        last = mm(pYT[:, g * E:(g + 1) * E], n3T[:, b, g, :], gatew_sb[:, :], start=True, stop=True)
                    last.then_inc(S["Lp"], 1)
            pipeline(pe, step)

            pe.wait_ge(S["slott"], PAIRS)
            pe.wait_ge(S["seen"], PAIRS)
            pe.wait_ge(S["lg"], PAIRS)
            mm(bank[7][:, 0:NP], ones[:, :], seen[:, PAIRS % 4, :], start=True, stop=True).then_inc(s_cnt, 1)
            pe.wait_ge(s_tin, 1)
            for j in range(3):
                last = mm(bank[7][0:1, 128 + j * P:128 + (j + 1) * P], tinfo[:, j:j + 1], ident[:, :], start=True, stop=True)
            last.then_inc(s_descp, 1)
            pe.wait_ge(s_desc, 1)
            pe.wait_ge(s_w1, 16 * 4)
            pe.wait_ge(s_w1lo, 1)
            pe.wait_ge(s_w1hi, 1)

            def first_T(t, k):
                reached(pe, Q["nx"], t + 1)
                if k >= 2:
                    reached(pe, Q["xo"], t - 1)
                nc.tensor.transpose(bank[k % 2][:, 0:P], nx[:, k % R2, :], ident[:, :]).then_inc(Q["T1"], 1)

            def step2(t, k):
                if k == 0:
                    first_T(0, 0)
                if k < TILES:
                    r = k % R2
                    ea_ = pe.value_load(desc[0:1, ds(P + t, 1)], min_val=0, max_val=E - 1)
                    eb_ = pe.value_load(desc[0:1, ds(2 * P + t, 1)], min_val=0, max_val=E - 1)
                    reached(pe, Q["xo"], t + 1)
                    if k >= 2:
                        reached(pe, Q["hb"], t - 1)
                    o = bank[2 + k % 2]
                    for j, e in enumerate((ea_, eb_)):
                        oj = o[:, j * HID:(j + 1) * HID]
                        hi = w1_hi[:, ds(e * HID, HID)]
                        lo = w1_lo[:, ds(e * HID, HID)]
                        mm(oj, xo[:, r, :], hi, start=True, stop=False)
                        mm(oj, xh[:, r, :], lo, start=False, stop=False)
                        last = mm(oj, xh[:, r, :], hi, start=False, stop=True)
                    last.then_inc(Q["L1"], 1)
                if 1 <= k <= TILES:
                    r = (k - 1) % R2
                    reached(pe, Q["hg"], t)
                    if k >= 3:
                        reached(pe, Q["hT"], t - 2)
                    o = bank[4 + (k - 1) % 2]
                    for c in range(2 * KC):
                        last = nc.tensor.transpose(o[:, c * P:(c + 1) * P], hg[:, r, c * P:(c + 1) * P], ident[:, :])
                    last.then_inc(Q["Tg"], 1)
                if k + 1 < TILES:
                    first_T(t + 1, k + 1)
                if k >= 2:
                    r = (k - 2) % R2
                    ea_ = pe.value_load(desc[0:1, ds(P + t - 2, 1)], min_val=0, max_val=E - 1)
                    eb_ = pe.value_load(desc[0:1, ds(2 * P + t - 2, 1)], min_val=0, max_val=E - 1)
                    reached(pe, Q["hT"], t - 1)
                    if k >= 4:
                        reached(pe, Q["ro"], t - 3)
                    o = bank[6 + (k - 2) % 2]
                    w2f = w2_sb[:, :, :].rearrange("p c d -> p (c d)")
                    for j, e in enumerate((ea_, eb_)):
                        for c in range(KC):
                            last = mm(o[:, j * D:(j + 1) * D], hT[:, r, j * KC + c, :],
                                      w2f[:, ds(e * (KC * D) + c * D, D)], start=(c == 0), stop=(c == KC - 1))
                    last.then_inc(Q["L2"], 1)

            tiles_skewed(pe, step2)

        @block.scalar
        def _(act):
            fn = nc.scalar.activation

            def evac_norm(i, k):
                b = k % 2
                reached(act, S["nTp"], i + 1)
                if k >= 2:
                    reached(act, S["Xp"], i - 1)
                fn(nrmT[:, b, :, :], pQK[:, 0:GD].rearrange("p (g n) -> p g n", g=G), ACT.Copy).then_inc(S["nrmT"], 1)

            def step(i, k):
                if k == 0:
                    evac_norm(0, 0)
                if isinstance(i, int) and i == HI_AT:
                    act.wait_ge(s_w1, 16 * 4)
                    fn(w1_hi[:, :], w1_sb[:, :], ACT.Copy).then_inc(s_w1hi, 1)
                if live(k, 0):
                    b = k % 2
                    reached(act, S["qk"], i + 1)
                    if k >= 2:
                        reached(act, S["qkl"], i - 1)
                    fn(qkc[:, b, :, :, :].rearrange("p a g n -> p (a g n)"), pQK[:, :], ACT.Copy).then_inc(S["qkc"], 1)
                if live(k, 1):
                    b = (k - 1) % 2
                    reached(act, S["Ep"], i)
                    if k >= 3:
                        reached(act, S["YTp"], i - 2)
                    for g in range(G):
                        last = fn(adjhT[:, b, g, :, :], pE[g][:, :].rearrange("p (h n) -> p h n", h=H), ACT.Copy)
                    last.then_inc(S["adjhT"], 1)
                if live(k, 0):
                    b = k % 2
                    reached(act, S["qkl"], i + 1)
                    if k >= 2:
                        reached(act, S["S"], i - 1)
                    for h in range(H):
                        rng = slice(h * HD, (h + 1) * HD)
                        last = fn(qbd[rng, b, :, h, :], qkl[rng, b, 0, :, :], ACT.Copy)
                    last.then_inc(S["qT"], 1)
                    reached(act, S["S"], i + 1)
                    if k >= 2:
                        reached(act, S["adjh"], i - 1)
                    for g in range(G):
                        last = fn(att[:, b, g, :, :], pS[g][:, :].rearrange("p (h n) -> p h n", h=H), ACT.Sigmoid, scale=SCALE)
                    last.then_inc(S["att"], 1)
                if live(k, 1):
                    b = (k - 1) % 2
                    reached(act, S["YTp"], i)
                    if k >= 3:
                        reached(act, S["Yp"], i - 2)
                    fn(yT[:, b, :, :], pYT[:, 0:GD].rearrange("p (g n) -> p g n", g=G), ACT.Copy).then_inc(S["yT"], 1)
                if live(k + 1, 0):
                    evac_norm(i + 1, k + 1)
                if live(k, 2):
                    b = (k - 2) % 2
                    reached(act, S["n3Tp"], i - 1)
                    if k >= 4:
                        reached(act, S["Lp"], i - 3)
                    fn(n3T[:, b, :, :], pX[:, 0:GD].rearrange("p (g n) -> p g n", g=G), ACT.Copy).then_inc(S["n3T"], 1)
                if live(k, 3):
                    b = (k - 3) % 2
                    reached(act, S["zz"], i - 2)
                    if k >= 5:
                        reached(act, S["ez"], i - 4)
                    fn(sp[:, b, :, :], zz[:, b, :, :], ACT.Sigmoid).then_inc(S["sp"], 1)
                    fn(sn[:, b, :, :], zz[:, b, :, :], ACT.Sigmoid, scale=-1.0).then_inc(S["sn"], 1)

            act.wait_ge(s_const, 1)
            pipeline(act, step)

            def step2(t, k):
                if k < TILES:
                    r = k % R2
                    reached(act, Q["T1"], t + 1)
                    if k >= R2:
                        reached(act, Q["L1"], t - R2 + 1)
                    fn(xh[:, r, :], bank[k % 2][:, 0:P], ACT.Copy).then_inc(Q["xh"], 1)
                if k >= 1 and k - 1 < TILES:
                    r = (k - 1) % R2
                    reached(act, Q["hb"], t)
                    if k - 1 >= R2:
                        reached(act, Q["Tg"], t - R2)
                    fn(hg[:, r, :], hb[:, r, :], ACT.Gelu).then_inc(Q["hg"], 1)
                    reached(act, Q["Tg"], t)
                    if k - 1 >= R2:
                        reached(act, Q["L2"], t - R2)
                    fn(hT[:, r, :, :], bank[4 + (k - 1) % 2][:, :].rearrange("p (c n) -> p c n", c=2 * KC), ACT.Copy).then_inc(Q["hT"], 1)

            tiles_skewed(act, step2)

        @block.gpsimd
        def _(pool):
            gp = nc.gpsimd
            gp.memset(ident[:, :], 0.0).then_inc(s_iota_c, 1)
            gp.memset(before[:, :], 1.0)
            gp.memset(ones[:, :], 1.0)
            gp.memset(neg_half[:, :], -0.5)
            gp.memset(filler[:, :], 0.0)
            gp.memset(eps_t[:, :], EPS)
            gp.memset(rows[:, :, :, D:ROW], 0.0)
            gp.memset(seen[:, 0, :], 0.0)
            gp.memset(zero28[:, :], 0.0).then_inc(s_iota_c, 1)
            pool.wait_ge(s_iota_c, 2)
            gp.affine_select(out=ident[:, :], in_=ident[:, :], compare_op=ALU.not_equal, fill=1.0, base=0,
                             pattern=[[-1, P]], channel_multiplier=1)
            gp.affine_select(out=before[:, :], in_=before[:, :], compare_op=ALU.is_gt, fill=0.0, base=0,
                             pattern=[[1, P]], channel_multiplier=-1)
            gp.iota(pair_no[:, :], [[1, NP]], base=0, channel_multiplier=0, allow_small_or_imprecise_dtypes=True)
            gp.iota(node_no[:, :], [[N, GRAPHS]], base=0, channel_multiplier=1)
            gp.iota(part_no[:, :], [[1, 1]], base=0, channel_multiplier=1, allow_small_or_imprecise_dtypes=True)
            for b in range(1, E):
                gp.memset(tri[:, b - 1:b], float(b * (b - 1) // 2))
            gp.memset(filler[:, C_NODE:C_NODE + 1].bitcast(i32), NO_NODE).then_inc(s_iota, 1)

            def var_rstd(src, vtmp, dst, sem_in, sem_v, sem_out, i, k, lag, readers):
                b = (k - lag) % 2
                reached(pool, S[sem_in], i + 1 - lag)
                if k - lag >= 2:
                    reached(pool, S[readers], i - 1 - lag)
                gp.tensor_tensor(vtmp[:, b, :], src[:, b, :, 1], eps_t[:, :], ALU.add).then_inc(S[sem_v], 1)
                reached(pool, S[sem_v], i + 1 - lag)
                gp.tensor_tensor(dst[:, b, :], vtmp[:, b, :], neg_half[:, 0:G], ALU.pow).then_inc(S[sem_out], 1)

            def step(i, k):
                if k == 0:
                    var_rstd(mv1, ve1, rs1, "mv1", "ve1", "rs1", 0, 0, 0, "nrm")
                if live(k + 1, 0):
                    var_rstd(mv1, ve1, rs1, "mv1", "ve1", "rs1", i + 1, k + 1, 0, "nrm")
                if live(k, 1):
                    var_rstd(mv2, ve2, rs2, "mv2", "ve2", "rs2", i, k, 1, "yn")
                if live(k, 1):
                    var_rstd(mv3, ve3, rs3, "mv3", "ve3", "rs3", i, k, 1, "row")
                if live(k, 0):
                    b = k % 2
                    reached(pool, S["degc"], i + 1)
                    reached(pool, S["degm"], i + 1)
                    gp.tensor_tensor(degp[:, b, :], degc[:, b, :], neg_half[:, :], ALU.pow).then_inc(S["degp"], 1)
                    reached(pool, S["degp"], i + 1)
                    if live(k, 4):
                        reached(pool, S["yv"], i - 3)
                        reached(pool, S["xs"], i - 3)
                    gp.tensor_tensor(dis[:, k % 4, :], degp[:, b, :], degm[:, b, :], ALU.mult).then_inc(S["dis"], 1)
                if live(k, 4):
                    r = (k - 4) % 4
                    reached(pool, S["slot"], i - 3)
                    reached(pool, S["row"], i - 3)
                    reached_alone(pool, S["wa"], i - 3)
                    for g in range(G):
                        gp.indirect_dma_start(
                            out=slots, out_offset=bass.IndirectOffsetOnAxis(ap=slot[:, r, g:g + 1], axis=0),
                            in_=rows[:, r, g, :], in_offset=None, bounds_check=DUMMY_ROW + P - 1, oob_is_err=True,
                        ).then_inc(s_scat[r], 16)

            pipeline(pool, step)

            def store(t, k):
                r = k % R2
                reached(pool, Q["ro"], t + 1)
                reached_alone(pool, Q["rid"], t + 1)
                gp.indirect_dma_start(
                    out=out_rows, out_offset=bass.IndirectOffsetOnAxis(ap=rid[:, r:r + 1], axis=0),
                    in_=ro[:, r, :], in_offset=None, bounds_check=NODES - 1, oob_is_err=False,
                ).then_inc(q_out[r], 16)

            tiles(pool, store)
            for r in range(R2):
                pool.wait_ge(q_out[r], 16 * len(range(r, TILES, R2)))

        @block.vector
        def _(dve):
            v = nc.vector

            def bc(ap, shape):
                return ap.to_broadcast(shape)

            def norm_stats(i, k):
                b = k % 2
                dve.wait_ge(s_x[k % 4], ring_count(i, k, 16))
                if k >= 2:
                    reached(dve, S["ve1"], i - 1)
                for g in range(G):
                    last = v.bn_stats(st1[:, b, g, :], xin[:, k % 4, g, :])
                last.then_inc(S["st1"], 1)
                reached_alone(dve, S["st1"], i + 1)
                for g in range(G):
                    last = v.bn_aggr(mv1[:, b, g, :], st1[:, b, g, :])
                last.then_inc(S["mv1"], 1)

            def norm_x(i, k):
                b = k % 2
                reached(dve, S["rs1"], i + 1)
                if k >= 2:
                    reached(dve, S["nTp"], i - 1)
                for g in range(G):
                    last = v.tensor_scalar(nrm[:, b, g, :], xin[:, k % 4, g, :], mv1[:, b, g, 0:1], rs1[:, b, g:g + 1],
                                           ALU.subtract, ALU.mult)
                last.then_inc(S["nrm"], 1)

            def per_graph(t):
                return t.rearrange("p (g d) -> p g d", g=G)

            def step(i, k):
                if k == 0:
                    norm_stats(0, 0)
                    norm_x(0, 0)
                if isinstance(i, int) and i == LO_AT:
                    dve.wait_ge(s_w1hi, 1)
                    v.tensor_tensor(w1_lo[:, :], w1_sb[:, :], w1_hi[:, :].bitcast(f32), ALU.subtract).then_inc(s_w1lo, 1)
                if live(k, 0):
                    b = k % 2
                    reached(dve, S["qkc"], i + 1)
                    if k >= 2:
                        reached(dve, S["S"], i - 1)
                        reached(dve, S["qT"], i - 1)
                    qk_in = qkc[:, b, :, :, :].rearrange("p a g n -> p (a g n)")
                    v.scalar_tensor_tensor(qkl[:, b, :, :, :].rearrange("p a g n -> p (a g n)"), qk_in, LEAK, qk_in,
                                           ALU.mult, ALU.max).then_inc(S["qkl"], 1)
                    reached(dve, S["Xp"], i + 1)
                    v.tensor_tensor(xlb[:, b, :, :], per_graph(pX[:, 0:GD]), blin_bc[:, :].unsqueeze(1).to_broadcast([P, G, D]),
                                    ALU.add).then_inc(S["xlb"], 1)
                    reached(dve, S["xlb"], i + 1)
                    v.scalar_tensor_tensor(xl[:, b, :, :].rearrange("p g d -> p (g d)"), xlb[:, b, :, :].rearrange("p g d -> p (g d)"),
                                           LEAK, xlb[:, b, :, :].rearrange("p g d -> p (g d)"), ALU.mult, ALU.max).then_inc(S["xl"], 1)
                if live(k, 1):
                    b = (k - 1) % 2
                    reached(dve, S["dis"], i)
                    reached(dve, S["xl"], i)
                    if k >= 3:
                        reached(dve, S["YTp"], i - 2)
                    v.tensor_tensor(xs[:, b, :, :].rearrange("p g (h d) -> p (g h) d", h=H),
                                    xl[:, b, :, :].rearrange("p g (h d) -> p (g h) d", h=H),
                                    dis[:, (k - 1) % 4, :].unsqueeze(2).to_broadcast([P, GH, HD]), ALU.mult).then_inc(S["xs"], 1)
                if live(k + 1, 0):
                    norm_stats(i + 1, k + 1)
                if live(k, 3):
                    place(i, k)
                if live(k + 1, 0):
                    norm_x(i + 1, k + 1)
                if live(k, 1):
                    update_a(i, k)
                if live(k, 0):
                    edges(i, k, 0)
                if live(k, 1):
                    update_b(i, k)
                if live(k, 0):
                    edges(i, k, 1)
                if live(k, 1):
                    update_c(i, k)

            def edges(i, k, g):
                b = k % 2
                if g == 0:
                    reached(dve, S["att"], i + 1)
                    dve.wait_ge(s_adj[k % 4], ring_count(i, k, 16))
                    if k >= 2:
                        reached(dve, S["Ep"], i - 1)
                        reached(dve, S["degc"], i - 1)
                        reached(dve, S["degm"], i - 1)
                for h in range(H):
                    c = g * H + h
                    last = v.scalar_tensor_tensor(adjh[:, b, g, h, :], att[:, b, g, h, :], 1.0, adjin[:, k % 4, g, :],
                                                  ALU.mult, ALU.mult, accum_out=deg[:, b, c:c + 1])
                if g == G - 1:
                    last.then_inc(S["adjh"], 1)
                    reached(dve, S["adjh"], i + 1)
                    if k >= 2:
                        reached(dve, S["degp"], i - 1)
                        reached(dve, S["dis"], i - 1)
                    v.tensor_scalar(degc[:, b, :], deg[:, b, :], TINY, None, ALU.max).then_inc(S["degc"], 1)
                    v.tensor_scalar(degm[:, b, :], deg[:, b, :], 0.0, None, ALU.is_gt).then_inc(S["degm"], 1)

            def update_a(i, k):
                j, b, r = i - 1, (k - 1) % 2, (k - 1) % 4
                reached(dve, S["Yp"], j + 1)
                if k >= 3:
                    reached(dve, S["yn"], j - 1)
                    reached(dve, S["st2"], j - 1)
                v.tensor_tensor(yv[:, b, :, :].rearrange("p g (h d) -> p (g h) d", h=H),
                                pY[:, 0:GD].rearrange("p (c d) -> p c d", d=HD),
                                dis[:, r, :].unsqueeze(2).to_broadcast([P, GH, HD]), ALU.mult).then_inc(S["yv"], 1)
                reached(dve, S["yv"], j + 1)
                for g in range(G):
                    last = v.bn_stats(st2[:, b, g, :], yv[:, b, g, :])
                last.then_inc(S["st2"], 1)
                if k >= 3:
                    reached(dve, S["ve2"], j - 1)
                reached_alone(dve, S["st2"], j + 1)
                for g in range(G):
                    last = v.bn_aggr(mv2[:, b, g, :], st2[:, b, g, :])
                last.then_inc(S["mv2"], 1)
                v.tensor_tensor(xb[:, b, :, :], xin[:, r, :, :], lnb_bc[:, :].unsqueeze(1).to_broadcast([P, G, D]),
                                ALU.add).then_inc(S["xb"], 1)

            def update_b(i, k):
                j, b, r = i - 1, (k - 1) % 2, (k - 1) % 4
                reached(dve, S["rs2"], j + 1)
                for g in range(G):
                    last = v.tensor_scalar(yn[:, b, g, :], yv[:, b, g, :], mv2[:, b, g, 0:1], rs2[:, b, g:g + 1],
                                           ALU.subtract, ALU.mult)
                last.then_inc(S["yn"], 1)
                reached(dve, S["yn"], j + 1)
                v.tensor_tensor(yg[:, b, :, :], yn[:, b, :, :], lng_bc[:, :].unsqueeze(1).to_broadcast([P, G, D]),
                                ALU.mult).then_inc(S["yg"], 1)
                reached(dve, S["yg"], j + 1)
                reached(dve, S["xb"], j + 1)
                if k - 1 >= 4:
                    dve.wait_ge(s_scat[r], ring_count(j, k - 1, 32) - 32)
                v.tensor_tensor(rows[:, r, :, 0:D], yg[:, b, :, :], xb[:, b, :, :], ALU.add).then_inc(S["res"], 1)
                reached(dve, S["res"], j + 1)
                for g in range(G):
                    last = v.bn_stats(st3[:, b, g, :], rows[:, r, g, 0:D])
                last.then_inc(S["st3"], 1)
                if k >= 3:
                    reached(dve, S["ve3"], j - 1)
                reached_alone(dve, S["st3"], j + 1)
                for g in range(G):
                    last = v.bn_aggr(mv3[:, b, g, :], st3[:, b, g, :])
                last.then_inc(S["mv3"], 1)

            def update_c(i, k):
                j, b, r = i - 1, (k - 1) % 2, (k - 1) % 4
                reached(dve, S["mv3"], j + 1)
                reached(dve, S["rs3"], j + 1)
                if k >= 3:
                    reached(dve, S["n3Tp"], j - 1)
                for g in range(G):
                    last = v.tensor_scalar(n3[:, b, g, :], rows[:, r, g, 0:D], mv3[:, b, g, 0:1], rs3[:, b, g:g + 1],
                                           ALU.subtract, ALU.mult)
                last.then_inc(S["n3"], 1)
                v.tensor_copy(rows[:, r, :, C_MEAN:C_MEAN + 1], mv3[:, b, :, 0:1])
                v.tensor_copy(rows[:, r, :, C_RSTD:C_RSTD + 1], rs3[:, b, :].unsqueeze(2))
                v.tensor_copy(rows[:, r, :, C_NODE:C_NODE + 1].bitcast(i32),
                              node_no[:, ds(j * G, G)].unsqueeze(2)).then_inc(S["row"], 1)

            def gate(i, k):
                j, b, r = i - 2, (k - 2) % 2, (k - 2) % 4
                reached(dve, S["Lp"], j + 1)
                v.tensor_tensor(lg[:, b, :, :], pYT[:, 0:G * E].rearrange("p (g e) -> p g e", g=G),
                                gateb_bc[:, :].unsqueeze(1).to_broadcast([P, G, E]), ALU.add).then_inc(S["lg"], 1)
                reached_alone(dve, S["lg"], j + 1)
                for g in range(G):
                    last = v.max(mx[:, b, g, :], lg[:, b, g, :])
                last.then_inc(S["mx"], 1)
                reached(dve, S["mx"], j + 1)
                if k >= 4:
                    reached(dve, S["sn"], j - 1)
                    reached(dve, S["rank"], j - 1)
                v.tensor_tensor(zz[:, b, :, :], mx[:, b, :, :], mx[:, b, :, 0:1].to_broadcast([P, G, E]),
                                ALU.subtract).then_inc(S["zz"], 1)
                for g in range(G):
                    last = v.max_index(ix[:, b, g, :], mx[:, b, g, :], lg[:, b, g, :])
                last.then_inc(S["ix"], 1)
                reached(dve, S["ix"], j + 1)
                v.tensor_copy(ixf[:, b, :, :], ix[:, b, :, 0:2]).then_inc(S["ixf"], 1)
                reached(dve, S["ixf"], j + 1)
                v.tensor_tensor(ea[:, b, :], ixf[:, b, :, 0], ixf[:, b, :, 1], ALU.min).then_inc(S["ea"], 1)
                v.tensor_tensor(eb[:, b, :], ixf[:, b, :, 0], ixf[:, b, :, 1], ALU.max).then_inc(S["eb"], 1)
                v.tensor_tensor(sel[:, b, :], ixf[:, b, :, 0], ixf[:, b, :, 1], ALU.is_lt).then_inc(S["sel"], 1)
                reached(dve, S["eb"], j + 1)
                v.scalar_tensor_tensor(tb[:, b, :], eb[:, b, :], -1.0, eb[:, b, :], ALU.add, ALU.mult).then_inc(S["tb"], 1)
                reached(dve, S["tb"], j + 1)
                v.scalar_tensor_tensor(pid[:, b, :], tb[:, b, :], 0.5, ea[:, b, :], ALU.mult, ALU.add).then_inc(S["pid"], 1)
                reached(dve, S["pid"], j + 1)
                for g in range(G):
                    last = v.tensor_scalar(oh[:, b, g, :], pair_no[:, :], pid[:, b, g:g + 1], None, ALU.is_equal)
                last.then_inc(S["oh"], 1)
                v.tensor_scalar(base[:, b, :], pid[:, b, :], float(REGION), None, ALU.mult).then_inc(S["base"], 1)
                reached(dve, S["oh"], j + 1)
                v.tensor_tensor(seen1[:, b, :], seen[:, r, :], oh[:, b, 0, :], ALU.add).then_inc(S["seen1"], 1)
                reached(dve, S["seen1"], j + 1)
                v.tensor_tensor(seen[:, (r + 1) % 4, :], seen1[:, b, :], oh[:, b, 1, :], ALU.add).then_inc(S["seen"], 1)

            def weights(i, k):
                j, b, r = i - 3, (k - 3) % 2, (k - 3) % 4
                reached(dve, S["sn"], j + 1)
                v.reciprocal(rn[:, b, :, :], sn[:, b, :, :]).then_inc(S["rn"], 1)
                reached(dve, S["rn"], j + 1)
                reached(dve, S["sp"], j + 1)
                v.tensor_tensor(ez[:, b, :, :], sp[:, b, :, :], rn[:, b, :, :], ALU.mult).then_inc(S["ez"], 1)
                reached(dve, S["ez"], j + 1)
                v.tensor_reduce(es[:, b, :], ez[:, b, :, :], AX.X, ALU.add).then_inc(S["es"], 1)
                reached(dve, S["es"], j + 1)
                v.reciprocal(er[:, b, :], es[:, b, :]).then_inc(S["er"], 1)
                reached(dve, S["er"], j + 1)
                v.tensor_tensor(w12[:, b, :, :], ez[:, b, :, 0:2], er[:, b, :].unsqueeze(2).to_broadcast([P, G, 2]),
                                ALU.mult).then_inc(S["w12"], 1)
                reached(dve, S["w12"], j + 1)
                v.tensor_tensor(dw[:, b, :], w12[:, b, :, 0], w12[:, b, :, 1], ALU.subtract).then_inc(S["dw"], 1)
                reached(dve, S["dw"], j + 1)
                v.tensor_tensor(sdw[:, b, :], dw[:, b, :], sel[:, b, :], ALU.mult).then_inc(S["sdw"], 1)
                reached(dve, S["sdw"], j + 1)
                v.tensor_tensor(rows[:, r, :, C_WA], w12[:, b, :, 1], sdw[:, b, :], ALU.add)
                v.tensor_tensor(rows[:, r, :, C_WB], w12[:, b, :, 0], sdw[:, b, :], ALU.subtract).then_inc(S["wa"], 1)

            def place(i, k):
                j, b, r = i - 3, (k - 3) % 2, (k - 3) % 4
                reached(dve, S["rank"], j + 1)
                for g in range(G):
                    last = v.scalar_tensor_tensor(slot_t[:, g, :], oh[:, b, g, :], 1.0, pY[:, GD + g * NP:GD + (g + 1) * NP],
                                                  ALU.mult, ALU.mult, accum_out=pos[:, b, g:g + 1])
                last.then_inc(S["slott"], 1)
                reached(dve, S["slott"], j + 1)
                reached(dve, S["base"], j + 1)
                v.tensor_tensor(slot[:, r, :], base[:, b, :], pos[:, b, :], ALU.add).then_inc(S["slot"], 1)

            dve.wait_ge(s_par, 16 * 8)
            dve.wait_ge(s_iota, 1)
            for b in range(2):
                last = v.memset(qbd[:, b, :, :, :], 0.0)
            last.then_inc(s_const, 1)
            dve.wait_ge(s_const, 1)
            def both(i, k):
                step(i, k)
                if live(k, 3):
                    weights(i, k)
                if live(k, 2):
                    gate(i, k)

            pipeline(dve, both)

            n_plan = [0]

            def then(ins):
                n_plan[0] += 1
                ins.then_inc(s_chain, 1)
                dve.wait_ge(s_chain, n_plan[0])

            dve.wait_ge(s_cnt, 1)
            then(v.tensor_copy(cnt[:, :], bank[7][:, 0:NP]))
            then(v.tensor_scalar(cnti[:, :], cnt[:, :], float(P - 1), None, ALU.add))
            v.scalar_tensor_tensor(padrow[:, :], pair_no[:, :], float(REGION), cnt[:, :], ALU.mult, ALU.add).then_inc(s_plan, 1)
            then(v.tensor_scalar(tilesi[:, :], cnti[:, :], P.bit_length() - 1, None, ALU.logical_shift_right))
            then(v.tensor_copy(tilesf[:, :], tilesi[:, :]))
            then(v.tensor_tensor_scan(cum[:, :], tilesf[:, :], zero28[:, :], 0.0, ALU.add, ALU.add))
            then(v.tensor_scalar(past[:, :], cum[:, :], part_no[:, 0:1], None, ALU.is_le))
            then(v.reduce_sum(tinfo[:, 3:4], past[:, :], AX.X))
            then(v.scalar_tensor_tensor(scr28[:, :], past[:, :], 1.0, tilesf[:, :], ALU.mult, ALU.mult, accum_out=tinfo[:, 4:5]))
            then(v.tensor_tensor(tinfo[:, 5:6], part_no[:, :], tinfo[:, 4:5], ALU.subtract))
            then(v.tensor_scalar(tinfo[:, 6:7], tinfo[:, 5:6], float(P), None, ALU.mult))
            then(v.scalar_tensor_tensor(tinfo[:, 7:8], tinfo[:, 3:4], float(REGION), tinfo[:, 6:7], ALU.mult, ALU.add))
            then(v.tensor_scalar(tinfo[:, 0:1], tinfo[:, 7:8], float(DUMMY_ROW), None, ALU.min))
            then(v.tensor_scalar(ge7[:, :], tri[:, :], tinfo[:, 3:4], None, ALU.is_le))
            then(v.reduce_sum(tinfo[:, 2:3], ge7[:, :], AX.X))
            then(v.scalar_tensor_tensor(tinfo[:, 4:5], tinfo[:, 2:3], -1.0, tinfo[:, 2:3], ALU.add, ALU.mult))
            v.scalar_tensor_tensor(tinfo[:, 1:2], tinfo[:, 4:5], -0.5, tinfo[:, 3:4], ALU.mult, ALU.add).then_inc(s_tin, 1)
            dve.wait_ge(s_descp, 1)
            v.tensor_copy(desc[0:1, :], bank[7][0:1, 128:128 + 3 * P]).then_inc(s_desc, 1)
            dve.wait_ge(s_desc, 1)

            def head2(t, k):
                r = k % R2
                dve.wait_ge(q_in[r], ring_count(t, k, 16))
                if k >= R2:
                    reached(dve, Q["T1"], t - R2 + 1)
                v.tensor_scalar(nx[:, r, :], rin[:, r, 0:D], rin[:, r, C_MEAN:C_MEAN + 1], rin[:, r, C_RSTD:C_RSTD + 1],
                                ALU.subtract, ALU.mult).then_inc(Q["nx"], 1)

            def step2(t, k):
                if k == 0:
                    head2(0, 0)
                if k < TILES:
                    r = k % R2
                    reached(dve, Q["xh"], t + 1)
                    if k >= R2:
                        reached(dve, Q["L1"], t - R2 + 1)
                    v.tensor_tensor(xo[:, r, :], bank[k % 2][:, 0:P], xh[:, r, :].bitcast(f32), ALU.subtract).then_inc(Q["xo"], 1)
                if k + 1 < TILES:
                    head2(t + 1, k + 1)
                if k >= 2:
                    r = (k - 2) % R2
                    ea_ = dve.value_load(desc[0:1, ds(P + t - 2, 1)], min_val=0, max_val=E - 1)
                    eb_ = dve.value_load(desc[0:1, ds(2 * P + t - 2, 1)], min_val=0, max_val=E - 1)
                    y = bank[6 + (k - 2) % 2]
                    wa_, wb_ = rin[:, r, C_WA:C_WA + 1], rin[:, r, C_WB:C_WB + 1]
                    v.scalar_tensor_tensor(ra[:, r, :], b2_bc[:, ds(ea_ * D, D)], wa_, rin[:, r, 0:D], ALU.mult, ALU.add).then_inc(Q["ra"], 1)
                    reached(dve, Q["ra"], t - 1)
                    v.scalar_tensor_tensor(rb[:, r, :], b2_bc[:, ds(eb_ * D, D)], wb_, ra[:, r, :], ALU.mult, ALU.add).then_inc(Q["rb"], 1)
                    reached(dve, Q["rb"], t - 1)
                    reached(dve, Q["L2"], t - 1)
                    v.scalar_tensor_tensor(rc[:, r, :], y[:, 0:D], wa_, rb[:, r, :], ALU.mult, ALU.add).then_inc(Q["rc"], 1)
                    if k - 2 >= R2:
                        dve.wait_ge(q_out[r], ring_count(t - 2, k - 2, 16) - 16)
                    v.tensor_copy(rid[:, r:r + 1], rin[:, r, C_NODE:C_NODE + 1].bitcast(i32)).then_inc(Q["rid"], 1)
                    reached(dve, Q["rc"], t - 1)
                    v.scalar_tensor_tensor(ro[:, r, :], y[:, D:2 * D], wb_, rc[:, r, :], ALU.mult, ALU.add).then_inc(Q["ro"], 1)
                if k < TILES:
                    r = k % R2
                    ea_ = dve.value_load(desc[0:1, ds(P + t, 1)], min_val=0, max_val=E - 1)
                    eb_ = dve.value_load(desc[0:1, ds(2 * P + t, 1)], min_val=0, max_val=E - 1)
                    o = bank[2 + k % 2]
                    reached(dve, Q["L1"], t + 1)
                    if k >= R2:
                        reached(dve, Q["hg"], t - R2 + 1)
                    for j, e in enumerate((ea_, eb_)):
                        last = v.tensor_tensor(hb[:, r, j * HID:(j + 1) * HID], o[:, j * HID:(j + 1) * HID],
                                               b1_bc[:, ds(e * HID, HID)], ALU.add)
                    last.then_inc(Q["hb"], 1)

            tiles_skewed(dve, step2)


_INS = ['x', 'adj', 'L0_gnn_W_lin', 'L0_gnn_b_lin', 'L0_gnn_W_q', 'L0_gnn_W_k', 'L0_gnn_ln_g', 'L0_gnn_ln_b',
        'L0_ffn_gate_w', 'L0_ffn_gate_b', 'L0_ffn_W1', 'L0_ffn_b1', 'L0_ffn_W2', 'L0_ffn_b2']
_OUTS = [((64, 128, 128), 'float32')]


def kernel(**inputs):
    import numpy as _np
    import concourse.bacc as _bacc
    from concourse import mybir as _mybir
    from concourse.bass_utils import run_bass_kernel_spmd as _run

    nc = _bacc.Bacc("TRN2", target_bir_lowering=False, num_devices=1)
    arrays, args = {}, []
    for name in _INS:
        a = _np.ascontiguousarray(inputs[name])
        arrays[f"in_{name}_dram"] = a
        args.append(nc.dram_tensor(f"in_{name}_dram", a.shape, _mybir.dt.from_np(a.dtype), kind="ExternalInput").ap())
    for i, (shape, dtype) in enumerate(_OUTS):
        dt = _mybir.dt.from_np(_np.dtype(dtype))
        args.append(nc.dram_tensor(f"out_{i}_dram", shape, dt, kind="ExternalOutput").ap())
    graph_block_kernel(nc, *args)
    r = _run(nc, [arrays], core_ids=[0])
    return r.results[0]["out_0_dram"]
```

```python
import concourse.bass as bass
from concourse import mybir
from contextlib import ExitStack


def graph_block_kernel(
    nc: bass.Bass,
    x: bass.AP,
    adj: bass.AP,
    w_lin: bass.AP,
    b_lin: bass.AP,
    w_q: bass.AP,
    w_k: bass.AP,
    ln_g: bass.AP,
    ln_b: bass.AP,
    gate_w: bass.AP,
    gate_b: bass.AP,
    w1: bass.AP,
    b1: bass.AP,
    w2: bass.AP,
    b2: bass.AP,
    out: bass.AP,
):
    f32 = mybir.dt.float32
    f32r = mybir.dt.float32r
    bf16 = mybir.dt.bfloat16
    i32 = mybir.dt.int32
    u32 = mybir.dt.uint32
    ALU = mybir.AluOpType
    ACT = mybir.ActivationFunctionType
    AX = mybir.AxisListType
    ds = bass.ds

    P = 128
    UNROLL = True
    GRAPHS, N, D = x.shape
    E = gate_w.shape[1]
    HID = w1.shape[2]
    H = 4
    HD = D // H
    SCALE = float(HD) ** -0.5
    LEAK = 0.01
    EPS = 1e-5
    TINY = 1.2e-38
    G = 2
    PAIRS = GRAPHS // G
    GD = G * D
    GH = G * H
    NODES = GRAPHS * N

    NP = E * (E - 1) // 2
    REGION = NODES + P
    DUMMY_ROW = NP * REGION
    TILES = (NODES + NP * (P - 1)) // P
    KC = HID // P
    ROW = D + 8
    C_WA, C_WB, C_MEAN, C_RSTD, C_NODE = D, D + 1, D + 2, D + 3, D + 4
    NO_NODE = 1 << 20

    x_t = x.rearrange("g n d -> n g d")
    adj_t = adj.rearrange("g n m -> n g m")
    out_rows = out.rearrange("g n d -> (g n) d")
    slots = nc.dram_tensor("slots", (DUMMY_ROW + P, ROW), f32).ap()

    ctx = ExitStack()
    with ctx:
        def sb(name, shape, dt=f32):
            return ctx.enter_context(nc.sbuf_tensor(name, shape, dt))

        def pb(name, shape, dt=f32):
            return ctx.enter_context(nc.psum_tensor(name, shape, dt))

        def sem(name):
            return ctx.enter_context(nc.semaphore(name))

        ident = sb("ident", [P, P])
        before = sb("before", [P, P], bf16)
        ones = sb("ones", [P, P], bf16)
        ones_f = sb("ones_f", [2 * 32, P])
        pair_no = sb("pair_no", [P, NP])
        pair_start = sb("pair_start", [P, NP])
        node_no = sb("node_no", [P, GRAPHS], i32)
        tri = sb("tri", [P, E - 1])
        part_no = sb("part_no", [P, 1])
        neg_half = sb("neg_half", [P, GH])
        eps_t = sb("eps_t", [P, G])
        wlin_sb = sb("wlin_sb", [D, D])
        wq_sb = sb("wq_sb", [D, D])
        wk_sb = sb("wk_sb", [D, D])
        gatew_sb = sb("gatew_sb", [D, E])
        blin_bc = sb("blin_bc", [P, D])
        lng_bc = sb("lng_bc", [P, D])
        lnb_bc = sb("lnb_bc", [P, D])
        gateb_bc = sb("gateb_bc", [P, E])
        w1_sb = sb("w1_sb", [D, E * HID])
        w1_hi = sb("w1_hi", [D, E * HID], f32r)
        w1_lo = sb("w1_lo", [D, E * HID], f32r)
        w2_sb = sb("w2_sb", [P, E * KC, D])
        LO = 32
        bias = sb("bias", [2 * LO, E * HID])
        bias_hl = sb("bias_hl", [2 * LO, E * HID], f32r)
        b2_bc = sb("b2_bc", [P, E * HID])
        ones_hl = sb("ones_hl", [2 * LO, P], f32r)
        filler = sb("filler", [P, ROW])

        xin = sb("xin", [P, 4, G, D])
        adjin = sb("adjin", [P, 4, G, N])
        st1 = sb("st1", [P, 2, G, 6])
        mv1 = sb("mv1", [P, 2, G, 2])
        ve1 = sb("ve1", [P, 2, G])
        rs1 = sb("rs1", [P, 2, G])
        nrm = sb("nrm", [P, 2, G, D])
        nrmT = sb("nrmT", [D, 2, G, N])
        qbd = sb("qbd", [D, 2, G, H, N])
        qkc = sb("qkc", [D, 2, 2, G, N])
        qkl = sb("qkl", [D, 2, 2, G, N])
        xlb = sb("xlb", [P, 2, G, D])
        xl = sb("xl", [P, 2, G, D])
        att = sb("att", [P, 2, G, H, N])
        adjh = sb("adjh", [P, 2, G, H, N])
        deg = sb("deg", [P, 2, GH])
        degm = sb("degm", [P, 2, GH])
        degc = sb("degc", [P, 2, GH])
        degp = sb("degp", [P, 2, GH])
        dis = sb("dis", [P, 4, GH])
        adjhT = sb("adjhT", [P, 2, G, H, N])
        xs = sb("xs", [P, 2, G, D])
        yT = sb("yT", [D, 2, G, N])
        yv = sb("yv", [P, 2, G, D])
        st2 = sb("st2", [P, 2, G, 6])
        mv2 = sb("mv2", [P, 2, G, 2])
        ve2 = sb("ve2", [P, 2, G])
        rs2 = sb("rs2", [P, 2, G])
        yn = sb("yn", [P, 2, G, D])
        yg = sb("yg", [P, 2, G, D])
        xb = sb("xb", [P, 2, G, D])
        rows = sb("rows", [P, 4, G, ROW])
        st3 = sb("st3", [P, 2, G, 6])
        mv3 = sb("mv3", [P, 2, G, 2])
        ve3 = sb("ve3", [P, 2, G])
        rs3 = sb("rs3", [P, 2, G])
        n3 = sb("n3", [P, 2, G, D])
        n3T = sb("n3T", [D, 2, G, N])
        lg = sb("lg", [P, 2, G, E])
        mx = sb("mx", [P, 2, G, E])
        ix = sb("ix", [P, 2, G, E], u32)
        zz = sb("zz", [P, 2, G, E])
        sp = sb("sp", [P, 2, G, E])
        sn = sb("sn", [P, 2, G, E])
        rn = sb("rn", [P, 2, G, E])
        ez = sb("ez", [P, 2, G, E])
        es = sb("es", [P, 2, G])
        er = sb("er", [P, 2, G])
        w12 = sb("w12", [P, 2, G, 2])
        ixf = sb("ixf", [P, 2, G, 2])
        ea = sb("ea", [P, 2, G])
        eb = sb("eb", [P, 2, G])
        tb = sb("tb", [P, 2, G])
        pid = sb("pid", [P, 2, G])
        sel = sb("sel", [P, 2, G])
        dw = sb("dw", [P, 2, G])
        sdw = sb("sdw", [P, 2, G])
        sw = sb("sw", [P, 2, G])
        oh = sb("oh", [P, 2, G, NP], bf16)
        seen = sb("seen", [P, 4, NP], bf16)
        seen1 = sb("seen1", [P, 2, NP], bf16)
        slot_t = sb("slot_t", [P, 2, NP])
        pos = sb("pos", [P, 2, G])
        base = sb("base", [P, 2, G])
        slot = sb("slot", [P, 4, G], u32)

        cnt = sb("cnt", [P, NP])
        cnti = sb("cnti", [P, NP], i32)
        tilesi = sb("tilesi", [P, NP], i32)
        tilesf = sb("tilesf", [P, NP])
        zero28 = sb("zero28", [P, NP])
        cum = sb("cum", [P, NP])
        past = sb("past", [P, NP])
        scr28 = sb("scr28", [P, NP])
        ge7 = sb("ge7", [P, E - 1])
        scr7 = sb("scr7", [P, E - 1])
        tinfo = sb("tinfo", [P, 8])
        padrow = sb("padrow", [P, NP], i32)
        desc = sb("desc", [1, 3 * P], i32)
        R2, RO, RIN = 4, 8, 16
        rin = sb("rin", [P, RIN, ROW])
        nx = sb("nx", [P, R2, D])
        xh = sb("xh", [D, R2, P], f32r)
        xo = sb("xo", [D, R2, P], f32r)
        hg = sb("hg", [P, R2, 2 * HID])
        hT = sb("hT", [P, R2, 2 * KC, P])
        ra = sb("ra", [P, R2, D])
        rb = sb("rb", [P, R2, D])
        rc = sb("rc", [P, R2, D])
        ro = sb("ro", [P, RO, D])

        bank = [pb(f"bank{i}", [P, 512]) for i in range(8)]
        pS = [bank[0], bank[1]]
        pE = [bank[2], bank[3]]
        pQK = bank[4]
        pX = bank[5]
        pYT = bank[6]
        pY = bank[7]

        s_const = sem("s_const")
        s_iota_c = sem("s_iota_c")
        s_chain = sem("s_chain")
        s_passed = {e: sem(f"s_passed_{n}") for n, e in (("dve", nc.vector.engine), ("pool", nc.gpsimd.engine))}
        s_iota = sem("s_iota")
        s_par = sem("s_par")
        s_w1 = sem("s_w1")
        s_w1hi = sem("s_w1hi")
        s_bz = sem("s_bz")
        s_bhl = sem("s_bhl")
        s_w1lo = sem("s_w1lo")
        s_x = [sem(f"s_x{r}") for r in range(4)]
        s_adj = [sem(f"s_adj{r}") for r in range(4)]
        names = ("st1 mv1 ve1 rs1 nrm nTp nrmT qk Xp qkc qkl qT xlb xl S att adjh degc degm degp dis "
                 "Ep adjhT xs YTp yT Yp yv st2 mv2 ve2 rs2 yn yg xb res st3 mv3 ve3 rs3 n3 n3Tp n3T "
                 "Lp lg mx ix zz sp sn rn ez es er w12 ixf ea eb tb pid sel dw sdw sw wa row "
                 "oh seen seen1 rank slott pos base slot").split()
        S = {n: sem("p_" + n) for n in names}
        s_scat = [sem(f"s_scat{r}") for r in range(4)]
        names2 = "nx T1 xh xo L1 hg Tg hT L2 ra rb rc ro".split()
        Q = {n: sem("q_" + n) for n in names2}
        q_in = [sem(f"q_in{r}") for r in range(RIN)]
        q_out = [sem(f"q_out{r}") for r in range(RO)]
        s_cnt = sem("s_cnt")
        s_plan = sem("s_plan")
        s_tin = sem("s_tin")
        s_descp = sem("s_descp")
        s_desc = sem("s_desc")
        s_pad = sem("s_pad")

        block = ctx.enter_context(nc.Block())

        def reached(eng, s, v):
            if isinstance(v, int) and v <= 0:
                return
            eng.wait_ge(s, v)

        def reached_alone(eng, s, v):
            if isinstance(v, int):
                return reached(eng, s, v)
            eng.wait_ge(s, v)
            eng.sem_inc(s_passed[eng.engine], 1)

        STEPS = PAIRS + 4
        FIRST, BODY = 8, 4
        LOOPED = (PAIRS - 1 - FIRST) // BODY * BODY

        def pipeline(eng, step):
            for i in range(FIRST):
                step(i, i)
            if UNROLL:
                for i in range(FIRST, FIRST + LOOPED):
                    step(i, i)
            else:
              with eng.Fori(0, LOOPED // BODY) as turn:
                for k in range(BODY):
                    step(turn * BODY + (FIRST + k), FIRST + k)
            for i in range(FIRST + LOOPED, STEPS):
                step(i, i)

        def live(k, lag):
            return 0 <= k - lag < PAIRS

        WEIGHTS_AT, HI_AT, LO_AT = 2, 6, 7

        AHEAD, BEHIND = 3, 3
        T_FIRST, T_BODY = 8, RIN
        T_LOOPED = (TILES - AHEAD - T_FIRST) // T_BODY * T_BODY

        def tiles(eng, step):
            for t in range(-AHEAD, T_FIRST):
                step(t, t)
            if UNROLL:
                for t in range(T_FIRST, T_FIRST + T_LOOPED):
                    step(t, t)
            else:
              with eng.Fori(0, T_LOOPED // T_BODY) as turn:
                for k in range(T_BODY):
                    step(turn * T_BODY + (T_FIRST + k), T_FIRST + k)
            for t in range(T_FIRST + T_LOOPED, TILES + BEHIND):
                step(t, t)

        def has_tile(k):
            return 0 <= k < TILES

        def ring_count(i, k, per, ring=4):
            q = k % ring
            if isinstance(i, int):
                return per * ((i - q) // ring + 1)
            return (i - q) * (per // ring) + per

        SP_FILLS = 15

        def expert_offsets(eng, t):
            return [nc.values_load(desc[0:1, ds(j * P + t, 1)], engines=(eng.engine,), min_val=0, max_val=(E - 1) * HID,
                                   skip_runtime_bounds_check_because="the plan counts experts below E only")
                    for j in (1, 2)]

        def fill_regions(eng, regions):
            for p in regions:
                row = eng.value_load(padrow[0:1, p:p + 1], min_val=0, max_val=DUMMY_ROW)
                eng.dma_start(slots[ds(row, P), :], filler[:, :]).then_inc(s_pad, 16)

        @block.sync
        def _(sp_):
            for dst, src in ((wq_sb, w_q), (wk_sb, w_k), (wlin_sb, w_lin), (gatew_sb, gate_w)):
                sp_.dma_start(dst[:, :], src).then_inc(s_par, 16)
            for dst, src in ((blin_bc, b_lin), (lng_bc, ln_g), (lnb_bc, ln_b), (gateb_bc, gate_b)):
                sp_.dma_start(dst[:, :], src.partition_broadcast(P)).then_inc(s_par, 16)

            def step(i, k):
                if isinstance(i, int) and i == WEIGHTS_AT:
                    sp_.dma_start(w1_sb[:, :].rearrange("p (e h) -> p e h", e=E), w1.rearrange("e p h -> p e h")).then_inc(s_w1, 16)
                    sp_.dma_start(w2_sb[:, :, :], w2.rearrange("e (c p) d -> p (e c) d", p=P)).then_inc(s_w1, 16)
                    sp_.wait_ge(s_bz, 1)
                    for row in (0, LO):
                        sp_.dma_start(bias[row:row + 1, :], b1.rearrange("e h -> (e h)").unsqueeze(0)).then_inc(s_w1, 16)
                    sp_.dma_start(b2_bc[:, :].rearrange("p (e h) -> p e h", e=E)[:, :, 0:D], b2.partition_broadcast(P)).then_inc(s_w1, 16)
                if k + 2 >= PAIRS:
                    return
                r = (k + 2) % 4
                reached(sp_, S["xb"], (i - 1) if k - 1 > 0 else 0)
                reached(sp_, S["adjh"], (i - 1) if k - 1 > 0 else 0)
                sp_.dma_start(xin[:, r, :, :], x_t[:, ds((i + 2) * G, G), :]).then_inc(s_x[r], 16)
                sp_.dma_start(adjin[:, r, :, :], adj_t[:, ds((i + 2) * G, G), :]).then_inc(s_adj[r], 16)

            for p in range(2):
                sp_.dma_start(xin[:, p, :, :], x_t[:, p * G:(p + 1) * G, :]).then_inc(s_x[p], 16)
                sp_.dma_start(adjin[:, p, :, :], adj_t[:, p * G:(p + 1) * G, :]).then_inc(s_adj[p], 16)
            pipeline(sp_, step)

            sp_.wait_ge(s_plan, 1)
            fill_regions(sp_, range(0, SP_FILLS))
            sp_.dma_start(slots[DUMMY_ROW:DUMMY_ROW + P, :], filler[:, :]).then_inc(s_pad, 16)
            sp_.wait_ge(s_pad, 16 * (NP + 1))
            for r in range(4):
                sp_.wait_ge(s_scat[r], 16 * G * (PAIRS // 4))
            sp_.wait_ge(s_desc, 1)

            def load_tile(t, k):
                r = k % RIN
                if k >= RIN:
                    sp_.wait_ge(q_out[k % RO], ring_count(t - RIN, k - RIN, 16, RO))
                row = sp_.value_load(desc[0:1, ds(t, 1)], min_val=0, max_val=DUMMY_ROW)
                sp_.dma_start(rin[:, r, :], slots[ds(row, P), :]).then_inc(q_in[r], 16)

            def loads(t, k):
                if has_tile(k + 3):
                    load_tile(t + 3, k + 3)
            tiles(sp_, loads)

        @block.tensor
        def _(pe):
            mm = nc.tensor.matmul
            pe.wait_ge(s_const, 1)
            pe.wait_ge(s_iota, 1)
            pe.wait_ge(s_par, 16 * 8)

            def norm_T(i, k):
                b = k % 2
                reached(pe, S["nrm"], i + 1)
                reached(pe, S["qkc"], i)
                for g in range(G):
                    last = nc.tensor.transpose(pQK[:, g * N:(g + 1) * N], nrm[:, b, g, :], ident[:, :])
                last.then_inc(S["nTp"], 1)

            def step(i, k):
                if k == 0:
                    norm_T(0, 0)
                if live(k, 0):
                    b = k % 2
                    reached(pe, S["nrmT"], i + 1)
                    mm(pQK[:, 0:GD], wq_sb[:, :], nrmT[:, b, :, :].rearrange("p g n -> p (g n)"), start=True, stop=True)
                    mm(pQK[:, GD:2 * GD], wk_sb[:, :], nrmT[:, b, :, :].rearrange("p g n -> p (g n)"), start=True, stop=True).then_inc(S["qk"], 1)
                    if k >= 1:
                        reached(pe, S["xlb"], i)
                    if live(k, 3):
                        reached(pe, S["n3T"], i - 2)
                    for g in range(G):
                        last = mm(pX[:, g * D:(g + 1) * D], nrmT[:, b, g, :], wlin_sb[:, :], start=True, stop=True)
                    last.then_inc(S["Xp"], 1)
                if live(k, 1):
                    b = (k - 1) % 2
                    reached(pe, S["adjh"], i)
                    if k >= 2:
                        reached(pe, S["adjhT"], i - 1)
                    for g in range(G):
                        for h in range(H):
                            last = nc.tensor.transpose(pE[g][:, h * N:(h + 1) * N], adjh[:, b, g, h, :], ident[:, :])
                    last.then_inc(S["Ep"], 1)
                if live(k, 3):
                    b = (k - 3) % 2
                    reached(pe, S["oh"], i - 2)
                    reached(pe, S["seen"], i - 2)
                    reached(pe, S["yv"], min(i - 1, PAIRS) if isinstance(i, int) else i - 1)
                    for g in range(G):
                        o = pY[:, GD + g * NP:GD + (g + 1) * NP]
                        mm(o, before[:, :], oh[:, b, g, :], start=True, stop=False)
                        prior = seen[:, (k - 3) % 4, :] if g == 0 else seen1[:, b, :]
                        last = mm(o, ones[:, :], prior, start=False, stop=True)
                    last.then_inc(S["rank"], 1)
                if live(k, 0):
                    b = k % 2
                    reached(pe, S["qT"], i + 1)
                    if k >= 1:
                        reached(pe, S["att"], i)
                    for g in range(G):
                        for h in range(H):
                            last = mm(pS[g][:, h * N:(h + 1) * N], qbd[:, b, g, h, :], qkl[:, b, 1, g, :], start=True, stop=True)
                    last.then_inc(S["S"], 1)
                if live(k, 1):
                    b = (k - 1) % 2
                    reached(pe, S["adjhT"], i)
                    reached(pe, S["xs"], i)
                    if k >= 2:
                        reached(pe, S["yT"], i - 1)
                    if live(k, 3):
                        reached(pe, S["lg"], i - 2)
                    for g in range(G):
                        for h in range(H):
                            last = mm(pYT[h * HD:(h + 1) * HD, g * N:(g + 1) * N], xs[:, b, g, h * HD:(h + 1) * HD],
                                      adjhT[:, b, g, h, :], start=True, stop=True, skip_group_check=True)
                    last.then_inc(S["YTp"], 1)
                if live(k + 1, 0):
                    norm_T(i + 1, k + 1)
                if live(k, 2):
                    b = (k - 2) % 2
                    reached(pe, S["n3"], i - 1)
                    if live(k, 0):
                        reached(pe, S["xlb"], i + 1)
                    for g in range(G):
                        last = nc.tensor.transpose(pX[:, g * N:(g + 1) * N], n3[:, b, g, :], ident[:, :])
                    last.then_inc(S["n3Tp"], 1)
                if live(k, 1):
                    b = (k - 1) % 2
                    reached(pe, S["yT"], i)
                    if k >= 2:
                        reached(pe, S["yv"], i - 1)
                    if live(k, 3):
                        reached(pe, S["slott"], i - 2)
                    for g in range(G):
                        last = nc.tensor.transpose(pY[:, g * D:(g + 1) * D], yT[:, b, g, :], ident[:, :])
                    last.then_inc(S["Yp"], 1)
                if live(k, 2):
                    b = (k - 2) % 2
                    reached(pe, S["n3T"], i - 1)
                    if live(k, 1):
                        reached(pe, S["yT"], i)
                    if live(k, 3):
                        reached(pe, S["lg"], i - 2)
                    for g in range(G):
                        last = mm(pYT[:, g * E:(g + 1) * E], n3T[:, b, g, :], gatew_sb[:, :], start=True, stop=True)
                    last.then_inc(S["Lp"], 1)
            pipeline(pe, step)

            pe.wait_ge(S["slott"], PAIRS)
            pe.wait_ge(S["seen"], PAIRS)
            pe.wait_ge(S["lg"], PAIRS)
            mm(bank[7][:, 0:NP], ones[:, :], seen[:, PAIRS % 4, :], start=True, stop=True).then_inc(s_cnt, 1)
            pe.wait_ge(s_tin, 1)
            for j in range(3):
                last = mm(bank[7][0:1, 128 + j * P:128 + (j + 1) * P], tinfo[:, j:j + 1], ident[:, :], start=True, stop=True)
            last.then_inc(s_descp, 1)
            pe.wait_ge(s_desc, 1)
            pe.wait_ge(s_w1, 16 * 5)
            pe.wait_ge(s_w1lo, 1)
            pe.wait_ge(s_w1hi, 2)
            pe.wait_ge(s_bhl, 1)
            w2f = w2_sb[:, :, :].rearrange("p c d -> p (c d)")
            offsets = {}

            def step2(t, k):
                if has_tile(k):
                    r = k % R2
                    offsets[k] = expert_offsets(pe, t)
                    if k >= 2:
                        reached(pe, Q["hg"], t - 1)
                    reached(pe, Q["xo"], t + 1)
                    o = bank[2 + k % 2]
                    for j, e in enumerate(offsets[k]):
                        oj = o[:, j * HID:(j + 1) * HID]
                        hi = w1_hi[:, ds(e, HID)]
                        lo = w1_lo[:, ds(e, HID)]
                        mm(oj, ones_hl[:, :], bias_hl[:, ds(e, HID)], start=True, stop=False)
                        mm(oj, xo[:, r, :], hi, start=False, stop=False)
                        mm(oj, xh[:, r, :], hi, start=False, stop=False)
                        last = mm(oj, xh[:, r, :], lo, start=False, stop=True)
                    last.then_inc(Q["L1"], 1)
                if has_tile(k + 2):
                    if k >= 0:
                        reached(pe, Q["xo"], t + 1)
                    reached(pe, Q["nx"], t + 3)
                    nc.tensor.transpose(bank[k % 2][:, 0:P], nx[:, (k + 2) % R2, :], ident[:, :]).then_inc(Q["T1"], 1)
                if has_tile(k - 1):
                    if k >= 3:
                        reached(pe, Q["hT"], t - 2)
                    reached(pe, Q["hg"], t)
                    o = bank[4 + (k - 1) % 2]
                    for c in range(2 * KC):
                        last = nc.tensor.transpose(o[:, c * P:(c + 1) * P], hg[:, (k - 1) % R2, c * P:(c + 1) * P], ident[:, :])
                    last.then_inc(Q["Tg"], 1)
                if has_tile(k - 2):
                    r = (k - 2) % R2
                    if k >= 4:
                        reached(pe, Q["ro"], t - 3)
                    reached(pe, Q["hT"], t - 1)
                    o = bank[6 + k % 2]
                    for j, e in enumerate(offsets[k - 2]):
                        oj = o[:, j * D:(j + 1) * D]
                        for c in range(KC):
                            last = mm(oj, hT[:, r, j * KC + c, :], w2f[:, ds(e + c * D, D)], start=(c == 0), stop=(c == KC - 1))
                    last.then_inc(Q["L2"], 1)

            tiles(pe, step2)

        @block.scalar
        def _(act):
            fn = nc.scalar.activation

            def evac_norm(i, k):
                b = k % 2
                reached(act, S["nTp"], i + 1)
                if k >= 2:
                    reached(act, S["Xp"], i - 1)
                fn(nrmT[:, b, :, :], pQK[:, 0:GD].rearrange("p (g n) -> p g n", g=G), ACT.Copy).then_inc(S["nrmT"], 1)

            def step(i, k):
                if k == 0:
                    evac_norm(0, 0)
                if isinstance(i, int) and i == HI_AT:
                    act.wait_ge(s_w1, 16 * 5)
                    fn(w1_hi[:, :], w1_sb[:, :], ACT.Copy).then_inc(s_w1hi, 1)
                    fn(ones_hl[:, :], ones_f[:, :], ACT.Copy)
                    fn(bias_hl[:, :], bias[:, :], ACT.Copy).then_inc(s_w1hi, 1)
                if live(k, 0):
                    b = k % 2
                    reached(act, S["qk"], i + 1)
                    if k >= 2:
                        reached(act, S["qkl"], i - 1)
                    fn(qkc[:, b, :, :, :].rearrange("p a g n -> p (a g n)"), pQK[:, :], ACT.Copy).then_inc(S["qkc"], 1)
                if live(k, 1):
                    b = (k - 1) % 2
                    reached(act, S["Ep"], i)
                    if k >= 3:
                        reached(act, S["YTp"], i - 2)
                    for g in range(G):
                        last = fn(adjhT[:, b, g, :, :], pE[g][:, :].rearrange("p (h n) -> p h n", h=H), ACT.Copy)
                    last.then_inc(S["adjhT"], 1)
                if live(k, 0):
                    b = k % 2
                    reached(act, S["qkl"], i + 1)
                    if k >= 2:
                        reached(act, S["S"], i - 1)
                    for h in range(H):
                        rng = slice(h * HD, (h + 1) * HD)
                        last = fn(qbd[rng, b, :, h, :], qkl[rng, b, 0, :, :], ACT.Copy)
                    last.then_inc(S["qT"], 1)
                    reached(act, S["S"], i + 1)
                    if k >= 2:
                        reached(act, S["adjh"], i - 1)
                    for g in range(G):
                        last = fn(att[:, b, g, :, :], pS[g][:, :].rearrange("p (h n) -> p h n", h=H), ACT.Sigmoid, scale=SCALE)
                    last.then_inc(S["att"], 1)
                if live(k, 1):
                    b = (k - 1) % 2
                    reached(act, S["YTp"], i)
                    if k >= 3:
                        reached(act, S["Yp"], i - 2)
                    fn(yT[:, b, :, :], pYT[:, 0:GD].rearrange("p (g n) -> p g n", g=G), ACT.Copy).then_inc(S["yT"], 1)
                if live(k + 1, 0):
                    evac_norm(i + 1, k + 1)
                if live(k, 2):
                    b = (k - 2) % 2
                    reached(act, S["n3Tp"], i - 1)
                    if k >= 4:
                        reached(act, S["Lp"], i - 3)
                    fn(n3T[:, b, :, :], pX[:, 0:GD].rearrange("p (g n) -> p g n", g=G), ACT.Copy).then_inc(S["n3T"], 1)
                if live(k, 3):
                    b = (k - 3) % 2
                    reached(act, S["zz"], i - 2)
                    if k >= 5:
                        reached(act, S["ez"], i - 4)
                    fn(sp[:, b, :, :], zz[:, b, :, :], ACT.Sigmoid).then_inc(S["sp"], 1)
                    fn(sn[:, b, :, :], zz[:, b, :, :], ACT.Sigmoid, scale=-1.0).then_inc(S["sn"], 1)

            act.wait_ge(s_const, 1)
            pipeline(act, step)

            act.wait_ge(s_plan, 1)
            fill_regions(act, range(SP_FILLS, NP))

            def step2(t, k):
                if has_tile(k):
                    if k >= R2:
                        reached(act, Q["Tg"], t - R2 + 1)
                    reached(act, Q["L1"], t + 1)
                    fn(hg[:, k % R2, :], bank[2 + k % 2][:, :], ACT.Gelu).then_inc(Q["hg"], 1)
                if has_tile(k + 2):
                    if k + 2 >= R2:
                        reached(act, Q["L1"], t + 2 - R2 + 1)
                    reached(act, Q["T1"], t + 3)
                    fn(xh[:, (k + 2) % R2, :], bank[k % 2][:, 0:P], ACT.Copy).then_inc(Q["xh"], 1)
                if has_tile(k - 1):
                    if k - 1 >= R2:
                        reached(act, Q["L2"], t - R2)
                    reached(act, Q["Tg"], t)
                    fn(hT[:, (k - 1) % R2, :, :], bank[4 + (k - 1) % 2][:, :].rearrange("p (c n) -> p c n", c=2 * KC), ACT.Copy).then_inc(Q["hT"], 1)

            tiles(act, step2)

        @block.gpsimd
        def _(pool):
            gp = nc.gpsimd
            gp.memset(ident[:, :], 0.0).then_inc(s_iota_c, 1)
            gp.memset(before[:, :], 1.0)
            gp.memset(ones[:, :], 1.0)
            gp.memset(ones_f[:, :], 1.0)
            gp.memset(bias[:, :], 0.0).then_inc(s_bz, 1)
            gp.memset(neg_half[:, :], -0.5)
            gp.memset(filler[:, :], 0.0)
            gp.memset(eps_t[:, :], EPS)
            gp.memset(rows[:, :, :, D:ROW], 0.0)
            gp.memset(seen[:, 0, :], 0.0)
            gp.memset(zero28[:, :], 0.0).then_inc(s_iota_c, 1)
            pool.wait_ge(s_iota_c, 2)
            gp.affine_select(out=ident[:, :], in_=ident[:, :], compare_op=ALU.not_equal, fill=1.0, base=0,
                             pattern=[[-1, P]], channel_multiplier=1)
            gp.affine_select(out=before[:, :], in_=before[:, :], compare_op=ALU.is_gt, fill=0.0, base=0,
                             pattern=[[1, P]], channel_multiplier=-1)
            gp.iota(pair_no[:, :], [[1, NP]], base=0, channel_multiplier=0, allow_small_or_imprecise_dtypes=True)
            gp.iota(node_no[:, :], [[N, GRAPHS]], base=0, channel_multiplier=1)
            gp.iota(part_no[:, :], [[1, 1]], base=0, channel_multiplier=1, allow_small_or_imprecise_dtypes=True)
            for b in range(1, E):
                gp.memset(tri[:, b - 1:b], float(b * (b - 1) // 2))
            gp.memset(filler[:, C_NODE:C_NODE + 1].bitcast(i32), NO_NODE).then_inc(s_iota, 1)

            def var_rstd(src, vtmp, dst, sem_in, sem_v, sem_out, i, k, lag, readers):
                b = (k - lag) % 2
                reached(pool, S[sem_in], i + 1 - lag)
                if k - lag >= 2:
                    reached(pool, S[readers], i - 1 - lag)
                gp.tensor_tensor(vtmp[:, b, :], src[:, b, :, 1], eps_t[:, :], ALU.add).then_inc(S[sem_v], 1)
                reached(pool, S[sem_v], i + 1 - lag)
                gp.tensor_tensor(dst[:, b, :], vtmp[:, b, :], neg_half[:, 0:G], ALU.pow).then_inc(S[sem_out], 1)

            def step(i, k):
                if k == 0:
                    var_rstd(mv1, ve1, rs1, "mv1", "ve1", "rs1", 0, 0, 0, "nrm")
                if live(k + 1, 0):
                    var_rstd(mv1, ve1, rs1, "mv1", "ve1", "rs1", i + 1, k + 1, 0, "nrm")
                if live(k, 1):
                    var_rstd(mv2, ve2, rs2, "mv2", "ve2", "rs2", i, k, 1, "yn")
                if live(k, 1):
                    var_rstd(mv3, ve3, rs3, "mv3", "ve3", "rs3", i, k, 1, "row")
                if live(k, 0):
                    b = k % 2
                    reached(pool, S["degc"], i + 1)
                    reached(pool, S["degm"], i + 1)
                    gp.tensor_tensor(degp[:, b, :], degc[:, b, :], neg_half[:, :], ALU.pow).then_inc(S["degp"], 1)
                    reached(pool, S["degp"], i + 1)
                    if live(k, 4):
                        reached(pool, S["yv"], i - 3)
                        reached(pool, S["xs"], i - 3)
                    gp.tensor_tensor(dis[:, k % 4, :], degp[:, b, :], degm[:, b, :], ALU.mult).then_inc(S["dis"], 1)
                if live(k, 4):
                    r = (k - 4) % 4
                    reached(pool, S["slot"], i - 3)
                    reached(pool, S["row"], i - 3)
                    reached_alone(pool, S["wa"], i - 3)
                    for g in range(G):
                        gp.indirect_dma_start(
                            out=slots, out_offset=bass.IndirectOffsetOnAxis(ap=slot[:, r, g:g + 1], axis=0),
                            in_=rows[:, r, g, :], in_offset=None, bounds_check=DUMMY_ROW + P - 1, oob_is_err=True,
                        ).then_inc(s_scat[r], 16)

            pipeline(pool, step)

            def store(t, k):
                if has_tile(k - 3):
                    r = (k - 3) % RIN
                    reached_alone(pool, Q["ro"], t - 2)
                    gp.indirect_dma_start(
                        out=out_rows, out_offset=bass.IndirectOffsetOnAxis(ap=rin[:, r, C_NODE:C_NODE + 1].bitcast(u32), axis=0),
                        in_=ro[:, (k - 3) % RO, :], in_offset=None, bounds_check=NODES - 1, oob_is_err=False,
                    ).then_inc(q_out[(k - 3) % RO], 16)

            tiles(pool, store)
            for r in range(RO):
                pool.wait_ge(q_out[r], 16 * len(range(r, TILES, RO)))

        @block.vector
        def _(dve):
            v = nc.vector

            def bc(ap, shape):
                return ap.to_broadcast(shape)

            def norm_stats(i, k):
                b = k % 2
                dve.wait_ge(s_x[k % 4], ring_count(i, k, 16))
                if k >= 2:
                    reached(dve, S["ve1"], i - 1)
                for g in range(G):
                    last = v.bn_stats(st1[:, b, g, :], xin[:, k % 4, g, :])
                last.then_inc(S["st1"], 1)
                reached_alone(dve, S["st1"], i + 1)
                for g in range(G):
                    last = v.bn_aggr(mv1[:, b, g, :], st1[:, b, g, :])
                last.then_inc(S["mv1"], 1)

            def norm_x(i, k):
                b = k % 2
                reached(dve, S["rs1"], i + 1)
                if k >= 2:
                    reached(dve, S["nTp"], i - 1)
                for g in range(G):
                    last = v.tensor_scalar(nrm[:, b, g, :], xin[:, k % 4, g, :], mv1[:, b, g, 0:1], rs1[:, b, g:g + 1],
                                           ALU.subtract, ALU.mult)
                last.then_inc(S["nrm"], 1)

            def per_graph(t):
                return t.rearrange("p (g d) -> p g d", g=G)

            def step(i, k):
                if k == 0:
                    norm_stats(0, 0)
                    norm_x(0, 0)
                if isinstance(i, int) and i == LO_AT:
                    dve.wait_ge(s_w1hi, 2)
                    v.tensor_tensor(w1_lo[:, :], w1_sb[:, :], w1_hi[:, :].bitcast(f32), ALU.subtract).then_inc(s_w1lo, 1)
                    v.tensor_tensor(bias_hl[LO:LO + 1, :], bias[LO:LO + 1, :], bias_hl[LO:LO + 1, :].bitcast(f32),
                                    ALU.subtract).then_inc(s_bhl, 1)
                if live(k, 0):
                    b = k % 2
                    reached(dve, S["qkc"], i + 1)
                    if k >= 2:
                        reached(dve, S["S"], i - 1)
                        reached(dve, S["qT"], i - 1)
                    qk_in = qkc[:, b, :, :, :].rearrange("p a g n -> p (a g n)")
                    v.scalar_tensor_tensor(qkl[:, b, :, :, :].rearrange("p a g n -> p (a g n)"), qk_in, LEAK, qk_in,
                                           ALU.mult, ALU.max).then_inc(S["qkl"], 1)
                    reached(dve, S["Xp"], i + 1)
                    v.tensor_tensor(xlb[:, b, :, :], per_graph(pX[:, 0:GD]), blin_bc[:, :].unsqueeze(1).to_broadcast([P, G, D]),
                                    ALU.add).then_inc(S["xlb"], 1)
                    reached(dve, S["xlb"], i + 1)
                    v.scalar_tensor_tensor(xl[:, b, :, :].rearrange("p g d -> p (g d)"), xlb[:, b, :, :].rearrange("p g d -> p (g d)"),
                                           LEAK, xlb[:, b, :, :].rearrange("p g d -> p (g d)"), ALU.mult, ALU.max).then_inc(S["xl"], 1)
                if live(k, 1):
                    b = (k - 1) % 2
                    reached(dve, S["dis"], i)
                    reached(dve, S["xl"], i)
                    if k >= 3:
                        reached(dve, S["YTp"], i - 2)
                    v.tensor_tensor(xs[:, b, :, :].rearrange("p g (h d) -> p (g h) d", h=H),
                                    xl[:, b, :, :].rearrange("p g (h d) -> p (g h) d", h=H),
                                    dis[:, (k - 1) % 4, :].unsqueeze(2).to_broadcast([P, GH, HD]), ALU.mult).then_inc(S["xs"], 1)
                if live(k + 1, 0):
                    norm_stats(i + 1, k + 1)
                if live(k, 3):
                    place(i, k)
                if live(k + 1, 0):
                    norm_x(i + 1, k + 1)
                if live(k, 1):
                    update_a(i, k)
                if live(k, 0):
                    edges(i, k, 0)
                if live(k, 1):
                    update_b(i, k)
                if live(k, 0):
                    edges(i, k, 1)
                if live(k, 1):
                    update_c(i, k)

            def edges(i, k, g):
                b = k % 2
                if g == 0:
                    reached(dve, S["att"], i + 1)
                    dve.wait_ge(s_adj[k % 4], ring_count(i, k, 16))
                    if k >= 2:
                        reached(dve, S["Ep"], i - 1)
                        reached(dve, S["degc"], i - 1)
                        reached(dve, S["degm"], i - 1)
                for h in range(H):
                    c = g * H + h
                    last = v.scalar_tensor_tensor(adjh[:, b, g, h, :], att[:, b, g, h, :], 1.0, adjin[:, k % 4, g, :],
                                                  ALU.mult, ALU.mult, accum_out=deg[:, b, c:c + 1])
                if g == G - 1:
                    last.then_inc(S["adjh"], 1)
                    reached(dve, S["adjh"], i + 1)
                    if k >= 2:
                        reached(dve, S["degp"], i - 1)
                        reached(dve, S["dis"], i - 1)
                    v.tensor_scalar(degc[:, b, :], deg[:, b, :], TINY, None, ALU.max).then_inc(S["degc"], 1)
                    v.tensor_scalar(degm[:, b, :], deg[:, b, :], 0.0, None, ALU.is_gt).then_inc(S["degm"], 1)

            def update_a(i, k):
                j, b, r = i - 1, (k - 1) % 2, (k - 1) % 4
                reached(dve, S["Yp"], j + 1)
                if k >= 3:
                    reached(dve, S["yn"], j - 1)
                    reached(dve, S["st2"], j - 1)
                v.tensor_tensor(yv[:, b, :, :].rearrange("p g (h d) -> p (g h) d", h=H),
                                pY[:, 0:GD].rearrange("p (c d) -> p c d", d=HD),
                                dis[:, r, :].unsqueeze(2).to_broadcast([P, GH, HD]), ALU.mult).then_inc(S["yv"], 1)
                reached(dve, S["yv"], j + 1)
                for g in range(G):
                    last = v.bn_stats(st2[:, b, g, :], yv[:, b, g, :])
                last.then_inc(S["st2"], 1)
                if k >= 3:
                    reached(dve, S["ve2"], j - 1)
                reached_alone(dve, S["st2"], j + 1)
                for g in range(G):
                    last = v.bn_aggr(mv2[:, b, g, :], st2[:, b, g, :])
                last.then_inc(S["mv2"], 1)
                v.tensor_tensor(xb[:, b, :, :], xin[:, r, :, :], lnb_bc[:, :].unsqueeze(1).to_broadcast([P, G, D]),
                                ALU.add).then_inc(S["xb"], 1)

            def update_b(i, k):
                j, b, r = i - 1, (k - 1) % 2, (k - 1) % 4
                reached(dve, S["rs2"], j + 1)
                for g in range(G):
                    last = v.tensor_scalar(yn[:, b, g, :], yv[:, b, g, :], mv2[:, b, g, 0:1], rs2[:, b, g:g + 1],
                                           ALU.subtract, ALU.mult)
                last.then_inc(S["yn"], 1)
                reached(dve, S["yn"], j + 1)
                v.tensor_tensor(yg[:, b, :, :], yn[:, b, :, :], lng_bc[:, :].unsqueeze(1).to_broadcast([P, G, D]),
                                ALU.mult).then_inc(S["yg"], 1)
                reached(dve, S["yg"], j + 1)
                reached(dve, S["xb"], j + 1)
                if k - 1 >= 4:
                    dve.wait_ge(s_scat[r], ring_count(j, k - 1, 32) - 32)
                v.tensor_tensor(rows[:, r, :, 0:D], yg[:, b, :, :], xb[:, b, :, :], ALU.add).then_inc(S["res"], 1)
                reached(dve, S["res"], j + 1)
                for g in range(G):
                    last = v.bn_stats(st3[:, b, g, :], rows[:, r, g, 0:D])
                last.then_inc(S["st3"], 1)
                if k >= 3:
                    reached(dve, S["ve3"], j - 1)
                reached_alone(dve, S["st3"], j + 1)
                for g in range(G):
                    last = v.bn_aggr(mv3[:, b, g, :], st3[:, b, g, :])
                last.then_inc(S["mv3"], 1)

            def update_c(i, k):
                j, b, r = i - 1, (k - 1) % 2, (k - 1) % 4
                reached(dve, S["mv3"], j + 1)
                reached(dve, S["rs3"], j + 1)
                if k >= 3:
                    reached(dve, S["n3Tp"], j - 1)
                for g in range(G):
                    last = v.tensor_scalar(n3[:, b, g, :], rows[:, r, g, 0:D], mv3[:, b, g, 0:1], rs3[:, b, g:g + 1],
                                           ALU.subtract, ALU.mult)
                last.then_inc(S["n3"], 1)
                v.tensor_copy(rows[:, r, :, C_MEAN:C_MEAN + 1], mv3[:, b, :, 0:1])
                v.tensor_copy(rows[:, r, :, C_RSTD:C_RSTD + 1], rs3[:, b, :].unsqueeze(2))
                v.tensor_copy(rows[:, r, :, C_NODE:C_NODE + 1].bitcast(i32),
                              node_no[:, ds(j * G, G)].unsqueeze(2)).then_inc(S["row"], 1)

            def gate(i, k):
                j, b, r = i - 2, (k - 2) % 2, (k - 2) % 4
                reached(dve, S["Lp"], j + 1)
                v.tensor_tensor(lg[:, b, :, :], pYT[:, 0:G * E].rearrange("p (g e) -> p g e", g=G),
                                gateb_bc[:, :].unsqueeze(1).to_broadcast([P, G, E]), ALU.add).then_inc(S["lg"], 1)
                reached_alone(dve, S["lg"], j + 1)
                for g in range(G):
                    last = v.max(mx[:, b, g, :], lg[:, b, g, :])
                last.then_inc(S["mx"], 1)
                reached(dve, S["mx"], j + 1)
                if k >= 4:
                    reached(dve, S["sn"], j - 1)
                    reached(dve, S["rank"], j - 1)
                v.tensor_tensor(zz[:, b, :, :], mx[:, b, :, :], mx[:, b, :, 0:1].to_broadcast([P, G, E]),
                                ALU.subtract).then_inc(S["zz"], 1)
                for g in range(G):
                    last = v.max_index(ix[:, b, g, :], mx[:, b, g, :], lg[:, b, g, :])
                last.then_inc(S["ix"], 1)
                reached(dve, S["ix"], j + 1)
                v.tensor_copy(ixf[:, b, :, :], ix[:, b, :, 0:2]).then_inc(S["ixf"], 1)
                reached(dve, S["ixf"], j + 1)
                v.tensor_tensor(ea[:, b, :], ixf[:, b, :, 0], ixf[:, b, :, 1], ALU.min).then_inc(S["ea"], 1)
                v.tensor_tensor(eb[:, b, :], ixf[:, b, :, 0], ixf[:, b, :, 1], ALU.max).then_inc(S["eb"], 1)
                v.tensor_tensor(sel[:, b, :], ixf[:, b, :, 0], ixf[:, b, :, 1], ALU.is_lt).then_inc(S["sel"], 1)
                reached(dve, S["eb"], j + 1)
                v.scalar_tensor_tensor(tb[:, b, :], eb[:, b, :], -1.0, eb[:, b, :], ALU.add, ALU.mult).then_inc(S["tb"], 1)
                reached(dve, S["tb"], j + 1)
                v.scalar_tensor_tensor(pid[:, b, :], tb[:, b, :], 0.5, ea[:, b, :], ALU.mult, ALU.add).then_inc(S["pid"], 1)
                reached(dve, S["pid"], j + 1)
                for g in range(G):
                    last = v.tensor_scalar(oh[:, b, g, :], pair_no[:, :], pid[:, b, g:g + 1], None, ALU.is_equal)
                last.then_inc(S["oh"], 1)
                v.tensor_scalar(base[:, b, :], pid[:, b, :], float(REGION), None, ALU.mult).then_inc(S["base"], 1)
                reached(dve, S["oh"], j + 1)
                v.tensor_tensor(seen1[:, b, :], seen[:, r, :], oh[:, b, 0, :], ALU.add).then_inc(S["seen1"], 1)
                reached(dve, S["seen1"], j + 1)
                v.tensor_tensor(seen[:, (r + 1) % 4, :], seen1[:, b, :], oh[:, b, 1, :], ALU.add).then_inc(S["seen"], 1)

            def weights(i, k):
                j, b, r = i - 3, (k - 3) % 2, (k - 3) % 4
                reached(dve, S["sn"], j + 1)
                v.reciprocal(rn[:, b, :, :], sn[:, b, :, :]).then_inc(S["rn"], 1)
                reached(dve, S["rn"], j + 1)
                reached(dve, S["sp"], j + 1)
                v.tensor_tensor(ez[:, b, :, :], sp[:, b, :, :], rn[:, b, :, :], ALU.mult).then_inc(S["ez"], 1)
                reached(dve, S["ez"], j + 1)
                v.tensor_reduce(es[:, b, :], ez[:, b, :, :], AX.X, ALU.add).then_inc(S["es"], 1)
                reached(dve, S["es"], j + 1)
                v.reciprocal(er[:, b, :], es[:, b, :]).then_inc(S["er"], 1)
                reached(dve, S["er"], j + 1)
                v.tensor_tensor(w12[:, b, :, :], ez[:, b, :, 0:2], er[:, b, :].unsqueeze(2).to_broadcast([P, G, 2]),
                                ALU.mult).then_inc(S["w12"], 1)
                reached(dve, S["w12"], j + 1)
                v.tensor_tensor(dw[:, b, :], w12[:, b, :, 0], w12[:, b, :, 1], ALU.subtract).then_inc(S["dw"], 1)
                reached(dve, S["dw"], j + 1)
                v.tensor_tensor(sdw[:, b, :], dw[:, b, :], sel[:, b, :], ALU.mult).then_inc(S["sdw"], 1)
                reached(dve, S["sdw"], j + 1)
                v.tensor_tensor(rows[:, r, :, C_WA], w12[:, b, :, 1], sdw[:, b, :], ALU.add)
                v.tensor_tensor(rows[:, r, :, C_WB], w12[:, b, :, 0], sdw[:, b, :], ALU.subtract).then_inc(S["wa"], 1)

            def place(i, k):
                j, b, r = i - 3, (k - 3) % 2, (k - 3) % 4
                reached(dve, S["rank"], j + 1)
                for g in range(G):
                    last = v.scalar_tensor_tensor(slot_t[:, g, :], oh[:, b, g, :], 1.0, pY[:, GD + g * NP:GD + (g + 1) * NP],
                                                  ALU.mult, ALU.mult, accum_out=pos[:, b, g:g + 1])
                last.then_inc(S["slott"], 1)
                reached(dve, S["slott"], j + 1)
                reached(dve, S["base"], j + 1)
                v.tensor_tensor(slot[:, r, :], base[:, b, :], pos[:, b, :], ALU.add).then_inc(S["slot"], 1)

            dve.wait_ge(s_par, 16 * 8)
            dve.wait_ge(s_iota, 1)
            for b in range(2):
                last = v.memset(qbd[:, b, :, :, :], 0.0)
            last.then_inc(s_const, 1)
            dve.wait_ge(s_const, 1)
            def both(i, k):
                step(i, k)
                if live(k, 3):
                    weights(i, k)
                if live(k, 2):
                    gate(i, k)

            pipeline(dve, both)

            n_plan = [0]

            def then(ins):
                n_plan[0] += 1
                ins.then_inc(s_chain, 1)
                dve.wait_ge(s_chain, n_plan[0])

            dve.wait_ge(s_cnt, 1)
            then(v.tensor_copy(cnt[:, :], bank[7][:, 0:NP]))
            then(v.tensor_scalar(cnti[:, :], cnt[:, :], float(P - 1), None, ALU.add))
            v.scalar_tensor_tensor(padrow[:, :], pair_no[:, :], float(REGION), cnt[:, :], ALU.mult, ALU.add).then_inc(s_plan, 1)
            then(v.tensor_scalar(tilesi[:, :], cnti[:, :], P.bit_length() - 1, None, ALU.logical_shift_right))
            then(v.tensor_copy(tilesf[:, :], tilesi[:, :]))
            then(v.tensor_tensor_scan(cum[:, :], tilesf[:, :], zero28[:, :], 0.0, ALU.add, ALU.add))
            then(v.tensor_scalar(past[:, :], cum[:, :], part_no[:, 0:1], None, ALU.is_le))
            then(v.reduce_sum(tinfo[:, 3:4], past[:, :], AX.X))
            then(v.scalar_tensor_tensor(scr28[:, :], past[:, :], 1.0, tilesf[:, :], ALU.mult, ALU.mult, accum_out=tinfo[:, 4:5]))
            then(v.tensor_tensor(tinfo[:, 5:6], part_no[:, :], tinfo[:, 4:5], ALU.subtract))
            then(v.tensor_scalar(tinfo[:, 6:7], tinfo[:, 5:6], float(P), None, ALU.mult))
            then(v.scalar_tensor_tensor(tinfo[:, 7:8], tinfo[:, 3:4], float(REGION), tinfo[:, 6:7], ALU.mult, ALU.add))
            then(v.tensor_scalar(tinfo[:, 0:1], tinfo[:, 7:8], float(DUMMY_ROW), None, ALU.min))
            then(v.tensor_scalar(ge7[:, :], tri[:, :], tinfo[:, 3:4], None, ALU.is_le))
            then(v.reduce_sum(tinfo[:, 2:3], ge7[:, :], AX.X))
            then(v.scalar_tensor_tensor(tinfo[:, 4:5], tinfo[:, 2:3], -1.0, tinfo[:, 2:3], ALU.add, ALU.mult))
            then(v.scalar_tensor_tensor(tinfo[:, 1:2], tinfo[:, 4:5], -0.5, tinfo[:, 3:4], ALU.mult, ALU.add))
            v.tensor_scalar(tinfo[:, 1:3], tinfo[:, 1:3], float(HID), None, ALU.mult).then_inc(s_tin, 1)
            dve.wait_ge(s_descp, 1)
            v.tensor_copy(desc[0:1, :], bank[7][0:1, 128:128 + 3 * P]).then_inc(s_desc, 1)
            dve.wait_ge(s_desc, 1)

            def step2(t, k):
                if has_tile(k - 3):
                    r = (k - 3) % RIN
                    y = bank[6 + (k - 3) % 2]
                    wa, wb = rin[:, r, C_WA:C_WA + 1], rin[:, r, C_WB:C_WB + 1]
                    q = r % R2
                    e_a, e_b = expert_offsets(dve, t - 3)
                    v.scalar_tensor_tensor(ra[:, q, :], b2_bc[:, ds(e_a, D)], wa, rin[:, r, 0:D],
                                           ALU.mult, ALU.add).then_inc(Q["ra"], 1)
                    reached(dve, Q["ra"], t - 2)
                    v.scalar_tensor_tensor(rb[:, q, :], b2_bc[:, ds(e_b, D)], wb, ra[:, q, :],
                                           ALU.mult, ALU.add).then_inc(Q["rb"], 1)
                    reached(dve, Q["rb"], t - 2)
                    reached(dve, Q["L2"], t - 2)
                    v.scalar_tensor_tensor(rc[:, q, :], y[:, 0:D], wa, rb[:, q, :],
                                           ALU.mult, ALU.add).then_inc(Q["rc"], 1)
                    reached(dve, Q["rc"], t - 2)
                    if k - 3 >= RO:
                        dve.wait_ge(q_out[(k - 3) % RO], ring_count(t - 3, k - 3, 16, RO) - 16)
                    v.scalar_tensor_tensor(ro[:, (k - 3) % RO, :], y[:, D:2 * D], wb, rc[:, q, :],
                                           ALU.mult, ALU.add).then_inc(Q["ro"], 1)
                if has_tile(k + 3):
                    r = (k + 3) % RIN
                    if k + 3 >= R2:
                        reached(dve, Q["T1"], t + 3 - R2 + 1)
                    dve.wait_ge(q_in[r], ring_count(t + 3, k + 3, 16, RIN))
                    v.tensor_scalar(nx[:, (k + 3) % R2, :], rin[:, r, 0:D], rin[:, r, C_MEAN:C_MEAN + 1],
                                    rin[:, r, C_RSTD:C_RSTD + 1], ALU.subtract, ALU.mult).then_inc(Q["nx"], 1)
                if has_tile(k + 2):
                    r = (k + 2) % R2
                    if k + 2 >= R2:
                        reached(dve, Q["L1"], t + 2 - R2 + 1)
                    reached(dve, Q["xh"], t + 3)
                    v.tensor_tensor(xo[:, r, :], bank[k % 2][:, 0:P], xh[:, r, :].bitcast(f32), ALU.subtract).then_inc(Q["xo"], 1)

            tiles(dve, step2)


_INS = ['x', 'adj', 'L0_gnn_W_lin', 'L0_gnn_b_lin', 'L0_gnn_W_q', 'L0_gnn_W_k', 'L0_gnn_ln_g', 'L0_gnn_ln_b',
        'L0_ffn_gate_w', 'L0_ffn_gate_b', 'L0_ffn_W1', 'L0_ffn_b1', 'L0_ffn_W2', 'L0_ffn_b2']
_OUTS = [((64, 128, 128), 'float32')]


def kernel(**inputs):
    import numpy as _np
    import concourse.bacc as _bacc
    from concourse import mybir as _mybir
    from concourse.bass_utils import run_bass_kernel_spmd as _run

    nc = _bacc.Bacc("TRN2", target_bir_lowering=False, num_devices=1)
    arrays, args = {}, []
    for name in _INS:
        a = _np.ascontiguousarray(inputs[name])
        arrays[f"in_{name}_dram"] = a
        args.append(nc.dram_tensor(f"in_{name}_dram", a.shape, _mybir.dt.from_np(a.dtype), kind="ExternalInput").ap())
    for i, (shape, dtype) in enumerate(_OUTS):
        dt = _mybir.dt.from_np(_np.dtype(dtype))
        args.append(nc.dram_tensor(f"out_{i}_dram", shape, dt, kind="ExternalOutput").ap())
    graph_block_kernel(nc, *args)
    r = _run(nc, [arrays], core_ids=[0])
    return r.results[0]["out_0_dram"]
```

```python
import concourse.bass as bass
from concourse import mybir
from contextlib import ExitStack


def graph_block_kernel(
    nc: bass.Bass,
    x: bass.AP,
    adj: bass.AP,
    w_lin: bass.AP,
    b_lin: bass.AP,
    w_q: bass.AP,
    w_k: bass.AP,
    ln_g: bass.AP,
    ln_b: bass.AP,
    gate_w: bass.AP,
    gate_b: bass.AP,
    w1: bass.AP,
    b1: bass.AP,
    w2: bass.AP,
    b2: bass.AP,
    out: bass.AP,
):
    f32 = mybir.dt.float32
    f32r = mybir.dt.float32r
    bf16 = mybir.dt.bfloat16
    i32 = mybir.dt.int32
    u32 = mybir.dt.uint32
    ALU = mybir.AluOpType
    ACT = mybir.ActivationFunctionType
    AX = mybir.AxisListType
    ds = bass.ds

    P = 128
    GRAPHS, N, D = x.shape
    E = gate_w.shape[1]
    HID = w1.shape[2]
    H = 4
    HD = D // H
    SCALE = float(HD) ** -0.5
    LEAK = 0.01
    EPS = 1e-5
    TINY = 1.2e-38
    G = 2
    PAIRS = GRAPHS // G
    GD = G * D
    GH = G * H
    NODES = GRAPHS * N

    NP = E * (E - 1) // 2
    REGION = NODES + P
    DUMMY_ROW = NP * REGION
    TILES = (NODES + NP * (P - 1)) // P
    KC = HID // P
    ROW = D + 8
    C_WA, C_WB, C_MEAN, C_VAR, C_RSTD, C_SHIFT, C_NODE = (D + c for c in range(7))
    NO_NODE = 1 << 20

    x_t = x.rearrange("g n d -> n g d")
    adj_t = adj.rearrange("g n m -> n g m")
    out_rows = out.rearrange("g n d -> (g n) d")
    slots = nc.dram_tensor("slots", (DUMMY_ROW + P, ROW), f32).ap()

    ctx = ExitStack()
    with ctx:
        def sb(name, shape, dt=f32):
            return ctx.enter_context(nc.sbuf_tensor(name, shape, dt))

        def pb(name, shape, dt=f32):
            return ctx.enter_context(nc.psum_tensor(name, shape, dt))

        def sem(name):
            return ctx.enter_context(nc.semaphore(name))

        ident = sb("ident", [P, P])
        before = sb("before", [P, P], bf16)
        ones = sb("ones", [P, P], bf16)
        ones_f = sb("ones_f", [1, P])
        warm = sb("warm", [1, 1])
        pair_no = sb("pair_no", [P, NP])
        node_no = sb("node_no", [P, GRAPHS], i32)
        tri = sb("tri", [P, E - 1])
        part_no = sb("part_no", [P, 1])
        neg_half = sb("neg_half", [P, GH])
        eps_t = sb("eps_t", [P, G])
        wlin_sb = sb("wlin_sb", [D, D])
        wq_sb = sb("wq_sb", [D, D])
        wk_sb = sb("wk_sb", [D, D])
        gatew_sb = sb("gatew_sb", [D, E])
        blin = sb("blin", [1, G, D])
        lng_bc = sb("lng_bc", [P, D])
        lnb_bc = sb("lnb_bc", [P, D])
        gateb = sb("gateb", [1, G, E])
        w1_sb = sb("w1_sb", [D, E * HID])
        w1_hi = sb("w1_hi", [D, E * HID], f32r)
        w1_lo = sb("w1_lo", [D, E * HID], f32r)
        w2_sb = sb("w2_sb", [P, E * KC, D])
        b1_bc = sb("b1_bc", [P, E * HID])
        b2_bc = sb("b2_bc", [P, E * HID])
        filler = sb("filler", [P, ROW])

        XR, AR, RR = 8, 6, 6
        xin = sb("xin", [P, XR, G, D])
        adjin = sb("adjin", [P, AR, G, N])
        st1 = sb("st1", [P, 2, G, 6])
        mv1 = sb("mv1", [P, 2, G, 2])
        ve1 = sb("ve1", [P, 2, G])
        rs1 = sb("rs1", [P, 2, G])
        lm1 = sb("lm1", [P, 2, G])
        sh1 = sb("sh1", [P, 2, G])
        nrm = sb("nrm", [P, 2, G, D])
        nrmT = sb("nrmT", [D, 2, G, N])
        qkc = sb("qkc", [D, 2, 2, G, N])
        qkl = sb("qkl", [D, 2, 2, G, N])
        qbd = sb("qbd", [D, 2, G, H, N])
        xc = sb("xc", [P, 2, G, D])
        xl = sb("xl", [P, 4, G, D])
        att = sb("att", [P, 2, G, H, N])
        adjh = sb("adjh", [P, 2, G, H, N])
        deg = sb("deg", [P, 2, GH])
        degm = sb("degm", [P, 2, GH])
        degc = sb("degc", [P, 2, GH])
        degp = sb("degp", [P, 2, GH])
        dis = sb("dis", [P, 4, GH])
        adjhT = sb("adjhT", [P, 2, G, H, N])
        xs = sb("xs", [P, 2, G, D])
        yT = sb("yT", [D, 2, G, N])
        yv = sb("yv", [P, 2, G, D])
        st2 = sb("st2", [P, 2, G, 6])
        mv2 = sb("mv2", [P, 2, G, 2])
        ve2 = sb("ve2", [P, 2, G])
        rs2 = sb("rs2", [P, 2, G])
        yg = sb("yg", [P, 2, G, D])
        xb = sb("xb", [P, 2, G, D])
        rows = sb("rows", [P, RR, G, ROW])
        st3 = sb("st3", [P, 2, G, 6])
        ve3 = sb("ve3", [P, 2, G])
        lm3 = sb("lm3", [P, 2, G])
        n3 = sb("n3", [P, 2, G, D])
        n3T = sb("n3T", [D, 2, G, N])
        mx = sb("mx", [P, 2, G, E])
        ix = sb("ix", [P, 2, G, E], u32)
        zz = sb("zz", [P, 2, G, E])
        sp = sb("sp", [P, 2, G, E])
        sn = sb("sn", [P, 2, G, E])
        rn = sb("rn", [P, 2, G, E])
        ez = sb("ez", [P, 2, G, E])
        es = sb("es", [P, 2, G])
        er = sb("er", [P, 2, G])
        w12 = sb("w12", [P, 2, G, 2])
        ea = sb("ea", [P, 2, G])
        eb = sb("eb", [P, 2, G])
        tb = sb("tb", [P, 2, G])
        pid = sb("pid", [P, 2, G])
        sel = sb("sel", [P, 2, G])
        dw = sb("dw", [P, 2, G])
        sdw = sb("sdw", [P, 2, G])
        oh = sb("oh", [P, 2, G, NP], bf16)
        seen = sb("seen", [P, 2, NP], bf16)
        seen1 = sb("seen1", [P, 2, NP], bf16)
        own = sb("own", [P, G, NP])
        pos = sb("pos", [P, 2, G])
        slot = sb("slot", [P, 4, G], u32)

        cnt = sb("cnt", [P, NP])
        cnti = sb("cnti", [P, NP], i32)
        tilesi = sb("tilesi", [P, NP], i32)
        tilesf = sb("tilesf", [P, NP])
        zero28 = sb("zero28", [P, NP])
        cum = sb("cum", [P, NP])
        past = sb("past", [P, NP])
        scr28 = sb("scr28", [P, NP])
        ge7 = sb("ge7", [P, E - 1])
        tinfo = sb("tinfo", [P, 8])
        tiles_used = sb("tiles_used", [P, 1], i32)
        padrow = sb("padrow", [P, NP], i32)
        desc = sb("desc", [1, 3 * P], i32)
        R2, RO, RIN = 4, 8, 16
        rin = sb("rin", [P, RIN, ROW])
        nx = sb("nx", [P, R2, D])
        xh = sb("xh", [D, R2, P], f32r)
        xo = sb("xo", [D, R2, P], f32r)
        hb = sb("hb", [P, R2, 2 * HID])
        hg = sb("hg", [P, R2, 2 * HID])
        hT = sb("hT", [P, R2, 2 * KC, P])
        ra = sb("ra", [P, R2, D])
        rb = sb("rb", [P, R2, D])
        rc = sb("rc", [P, R2, D])
        ro = sb("ro", [P, RO, D])

        bank = [pb(f"bank{i}", [P, 512]) for i in range(8)]
        pS = [bank[0], bank[1]]
        pE = [bank[2], bank[3]]
        pQK = bank[4]
        pX = bank[5]
        pYT = bank[6]
        pY = bank[7]

        s_const = sem("s_const")
        s_iota_c = sem("s_iota_c")
        s_chain = sem("s_chain")
        s_early = sem("s_early")
        s_iota = sem("s_iota")
        s_par = sem("s_par")
        s_par2 = sem("s_par2")
        s_w1 = sem("s_w1")
        s_bz = sem("s_bz")
        s_w1hi = sem("s_w1hi")
        s_w1lo = sem("s_w1lo")
        s_x = [sem(f"s_x{r}") for r in range(XR)]
        s_adj = [sem(f"s_adj{r}") for r in range(AR)]
        names = ("st1 mv1 ve1 rs1 sh1 nrm nTp nrmT qk Xp qkc ql kl qbd0 qbd1 qbd2 qbd3 xc xl S att adjh degc degm degp dis "
                 "Ep adjhT xs YTp yT Yp yv st2 mv2 ve2 rs2 yg xb res st3 mv3 ve3 rs3 sh3 n3 n3Tp n3T "
                 "Lp mx ix zz sp sn rn ez es er w12 ea eb tb pid sel dw sdw wa node "
                 "oh seen seen1 rank pos slot").split()
        S = {n: sem("p_" + n) for n in names}
        s_scat = [sem(f"s_scat{r}") for r in range(RR)]
        names2 = "nx T1 xh xo L1 hb hg Tg hT L2 ra rb rc ro".split()
        Q = {n: sem("q_" + n) for n in names2}
        q_in = [sem(f"q_in{r}") for r in range(RIN)]
        q_out = [sem(f"q_out{r}") for r in range(RO)]
        s_cnt = sem("s_cnt")
        s_plan = sem("s_plan")
        s_tin = sem("s_tin")
        s_descp = sem("s_descp")
        s_desc = sem("s_desc")
        s_pad_sp, s_pad_act, s_pad_pool = sem("s_pad_sp"), sem("s_pad_act"), sem("s_pad_pool")

        block = ctx.enter_context(nc.Block())

        def after(eng, name, j):
            if j >= 0:
                eng.wait_ge(S[name], min(j, PAIRS - 1) + 1)

        def tile_after(eng, name, t):
            eng.wait_ge(Q[name], t + 1)

        NORM, PROJ, ATT, AGG, RES, GATE, PLACE, SCAT = range(8)
        STEPS = PAIRS + SCAT

        def run(stage, j):
            if 0 <= j < PAIRS:
                stage(j)

        def arrived(j, ring, per=16):
            return per * (j // ring + 1)

        WEIGHTS_AT = 5

        AHEAD, BEHIND = 3, 4

        USUAL = NODES // P + NP // 2 + 4

        def tiles(eng, walk):
            walk(range(USUAL))
            used = nc.values_load(tiles_used[0:1, 0:1], engines=(eng.engine,), min_val=0, max_val=TILES,
                                  skip_runtime_bounds_check_because="no split of the nodes needs more than TILES")
            with eng.If(used > USUAL):
                walk(range(USUAL, TILES))

        def steps(span):
            return range(span.start - AHEAD, span.stop + BEHIND)

        SP_FILLS, ACT_FILLS, POOL_FILLS = range(0, 11), range(11, 21), range(21, NP)

        def fill_regions(eng, regions, padded):
            for p in regions:
                row = nc.values_load(padrow[0:1, p:p + 1], engines=(eng.engine,), min_val=0, max_val=DUMMY_ROW,
                                     skip_runtime_bounds_check_because="a region has a row for every node, and P more")
                eng.dma_start(slots[ds(row, P), :], filler[:, :]).then_inc(padded, 16)

        PACK = 1 << 16

        def expert_offsets(eng, t):
            both = nc.values_load(desc[0:1, ds(P + t, 1)], engines=(eng.engine,), min_val=0, max_val=(E - 1) * HID * (PACK + 1),
                                  skip_runtime_bounds_check_because="the plan counts experts below E only")
            a, b = both & (PACK - 1), both >> (PACK.bit_length() - 1)
            return [eng.snap(nc.s_assert_within(v, min_val=0, max_val=(E - 1) * HID,
                                                skip_runtime_bounds_check_because="the plan counts experts below E only"))
                    for v in (a, b)]

        @block.sync
        def _(sp_):
            sp_.dma_start(xin[:, 0, :, :], x_t[:, 0:G, :]).then_inc(s_x[0], 16)
            for dst, src in ((wq_sb, w_q), (wk_sb, w_k), (wlin_sb, w_lin)):
                sp_.dma_start(dst[:, :], src).then_inc(s_par, 16)

            for j in range(PAIRS):
                after(sp_, "xb", j - XR)
                if j > 0:
                    sp_.dma_start(xin[:, j % XR, :, :], x_t[:, j * G:(j + 1) * G, :]).then_inc(s_x[j % XR], 16)
                after(sp_, "adjh", j - AR)
                sp_.dma_start(adjin[:, j % AR, :, :], adj_t[:, j * G:(j + 1) * G, :]).then_inc(s_adj[j % AR], 16)
                if j == 1:
                    for dst, src in ((lng_bc, ln_g), (lnb_bc, ln_b)):
                        sp_.dma_start(dst[:, :], src.partition_broadcast(P)).then_inc(s_par2, 16)
                    sp_.dma_start(gatew_sb[:, :], gate_w).then_inc(s_par2, 16)
                    for g in range(G):
                        sp_.dma_start(gateb[:, g, :], gate_b.unsqueeze(0)).then_inc(s_par2, 16)
                if j == WEIGHTS_AT:
                    sp_.dma_start(w1_sb[:, :].rearrange("p (e h) -> p e h", e=E), w1.rearrange("e p h -> p e h")).then_inc(s_w1, 16)
                    sp_.dma_start(w2_sb[:, :, :], w2.rearrange("e (c p) d -> p (e c) d", p=P)).then_inc(s_w1, 16)
                    sp_.wait_ge(s_bz, 1)
                    sp_.dma_start(b1_bc[:, :], b1.rearrange("e h -> (e h)").partition_broadcast(P)).then_inc(s_w1, 16)
                    sp_.dma_start(b2_bc[:, :].rearrange("p (e h) -> p e h", e=E)[:, :, 0:D], b2.partition_broadcast(P)).then_inc(s_w1, 16)

            sp_.wait_ge(s_iota, 1)
            sp_.dma_start(slots[DUMMY_ROW:DUMMY_ROW + P, :], filler[:, :]).then_inc(s_pad_sp, 16)
            sp_.wait_ge(s_plan, 1)
            fill_regions(sp_, SP_FILLS, s_pad_sp)
            sp_.wait_ge(s_pad_sp, 16 * (len(SP_FILLS) + 1))
            sp_.wait_ge(s_pad_act, 16 * len(ACT_FILLS))
            sp_.wait_ge(s_pad_pool, 16 * len(POOL_FILLS))
            for r in range(RR):
                sp_.wait_ge(s_scat[r], 16 * G * len(range(r, PAIRS, RR)))
            sp_.wait_ge(s_desc, 1)

            def load(span):
                for t in span:
                    if t >= RIN:
                        sp_.wait_ge(q_out[t % RO], arrived(t - RIN, RO))
                    row = nc.values_load(desc[0:1, ds(t, 1)], engines=(sp_.engine,), min_val=0, max_val=DUMMY_ROW,
                                         skip_runtime_bounds_check_because="the plan caps it at DUMMY_ROW")
                    sp_.dma_start(rin[:, t % RIN, :], slots[ds(row, P), :]).then_inc(q_in[t % RIN], 16)

            tiles(sp_, load)

        @block.tensor
        def _(pe):
            mm = nc.tensor.matmul
            pe.wait_ge(s_const, 1)
            pe.wait_ge(s_early, 1)
            pe.wait_ge(s_par, 16 * 5)

            def project_qk(j):
                after(pe, "nrmT", j)
                nT = nrmT[:, j % 2, :, :].rearrange("p g n -> p (g n)")
                mm(pQK[:, 0:GD], wq_sb[:, :], nT, start=True, stop=True)
                mm(pQK[:, GD:2 * GD], wk_sb[:, :], nT, start=True, stop=True).then_inc(S["qk"], 1)

            def project_x(j):
                after(pe, "nrmT", j)
                after(pe, "n3T", j + PROJ - GATE - 1)
                mm(pX[:, 0:GD], ones_f[0:1, :], blin[:, :, :].rearrange("p g d -> p (g d)"), start=True, stop=False, skip_group_check=True)
                for g in range(G):
                    last = mm(pX[:, g * D:(g + 1) * D], nrmT[:, j % 2, g, :], wlin_sb[:, :], start=False, stop=True, skip_group_check=True)
                last.then_inc(S["Xp"], 1)

            def aggregate(j):
                b = j % 2
                after(pe, "adjhT", j)
                after(pe, "xs", j)
                after(pe, "ix", j + AGG - GATE - 1)
                for g in range(G):
                    for h in range(H):
                        last = mm(pYT[h * HD:(h + 1) * HD, g * N:(g + 1) * N], xs[:, b, g, h * HD:(h + 1) * HD],
                                  adjhT[:, b, g, h, :], start=True, stop=True, skip_group_check=True)
                last.then_inc(S["YTp"], 1)

            def rank(j):
                b = j % 2
                if j == 0:
                    pe.wait_ge(s_iota, 1)
                after(pe, "oh", j)
                after(pe, "seen1", j)
                after(pe, "yv", j + PLACE - RES)
                for g in range(G):
                    o = pY[:, GD + g * NP:GD + (g + 1) * NP]
                    mm(o, before[:, :], oh[:, b, g, :], start=True, stop=False)
                    prior = seen[:, b, :] if g == 0 else seen1[:, b, :]
                    last = mm(o, ones[:, :], prior, start=False, stop=True)
                last.then_inc(S["rank"], 1)

            def residual_T(j):
                b = j % 2
                after(pe, "n3", j)
                after(pe, "xc", j + GATE - PROJ)
                for g in range(G):
                    last = nc.tensor.transpose(pX[:, g * N:(g + 1) * N], n3[:, b, g, :], ident[:, :])
                last.then_inc(S["n3Tp"], 1)

            def norm_T(j):
                b = j % 2
                after(pe, "nrm", j)
                after(pe, "qkc", j - 1)
                for g in range(G):
                    last = nc.tensor.transpose(pQK[:, g * N:(g + 1) * N], nrm[:, b, g, :], ident[:, :])
                last.then_inc(S["nTp"], 1)

            def aggregate_T(j):
                b = j % 2
                after(pe, "yT", j)
                after(pe, "yv", j - 1)
                after(pe, "pos", j + AGG - PLACE)
                for g in range(G):
                    last = nc.tensor.transpose(pY[:, g * D:(g + 1) * D], yT[:, b, g, :], ident[:, :])
                last.then_inc(S["Yp"], 1)

            def logits(j):
                b = j % 2
                after(pe, "n3T", j)
                after(pe, "yT", j + GATE - AGG)
                if j == 0:
                    pe.wait_ge(s_par2, 16 * 5)
                mm(pYT[:, 0:G * E], ones_f[0:1, :], gateb[:, :, :].rearrange("p g e -> p (g e)"), start=True, stop=False, skip_group_check=True)
                for g in range(G):
                    o = pYT[:, g * E:(g + 1) * E]
                    last = mm(o, n3T[:, b, g, :], gatew_sb[:, :], start=False, stop=True, skip_group_check=True)
                last.then_inc(S["Lp"], 1)

            def edges_T(j):
                b = j % 2
                after(pe, "adjhT", j - 1)
                after(pe, "adjh", j)
                for g in range(G):
                    for h in range(H):
                        last = nc.tensor.transpose(pE[g][:, h * N:(h + 1) * N], adjh[:, b, g, h, :], ident[:, :])
                last.then_inc(S["Ep"], 1)

            def scores(j):
                b = j % 2
                after(pe, "att", j - 1)
                after(pe, "kl", j)
                for h in range(H):
                    after(pe, f"qbd{h}", j)
                    for g in range(G):
                        last = mm(pS[g][:, h * N:(h + 1) * N], qbd[:, b, g, h, :], qkl[:, b, 1, g, :], start=True, stop=True)
                last.then_inc(S["S"], 1)

            for i in range(STEPS):
                run(edges_T, i - AGG)
                run(project_qk, i - PROJ)
                run(project_x, i - PROJ)
                run(aggregate, i - AGG)
                run(rank, i - PLACE)
                run(scores, i - PROJ)
                run(residual_T, i - GATE)
                run(norm_T, i - NORM)
                run(aggregate_T, i - AGG)
                run(logits, i - GATE)

            after(pe, "pos", PAIRS - 1)
            after(pe, "seen", PAIRS - 1)
            after(pe, "ix", PAIRS - 1)
            mm(bank[7][:, 0:NP], ones[:, :], seen[:, PAIRS % 2, :], start=True, stop=True).then_inc(s_cnt, 1)
            pe.wait_ge(s_w1, 16 * 4)
            pe.wait_ge(s_tin, 1)
            for j in range(3):
                last = mm(bank[7][0:1, 128 + j * P:128 + (j + 1) * P], tinfo[:, j:j + 1], ident[:, :], start=True, stop=True)
            last.then_inc(s_descp, 1)
            pe.wait_ge(s_desc, 1)
            pe.wait_ge(s_w1hi, 1)
            pe.wait_ge(s_w1lo, 1)
            w2f = w2_sb[:, :, :].rearrange("p c d -> p (c d)")
            offsets = {}

            def step2(t, span):
                if t + 2 in span:
                    if t >= 0:
                        tile_after(pe, "xo", t)
                    tile_after(pe, "nx", t + 2)
                    nc.tensor.transpose(bank[t % 2][:, 0:P], nx[:, (t + 2) % R2, :], ident[:, :]).then_inc(Q["T1"], 1)
                if t in span:
                    offsets[t] = expert_offsets(pe, t)
                    if t >= 2:
                        tile_after(pe, "hb", t - 2)
                    tile_after(pe, "xo", t)
                    for j, e in enumerate(offsets[t]):
                        o = bank[2 + t % 2][:, j * HID:(j + 1) * HID]
                        mm(o, xo[:, t % R2, :], w1_hi[:, ds(e, HID)], start=True, stop=False)
                        mm(o, xh[:, t % R2, :], w1_hi[:, ds(e, HID)], start=False, stop=False)
                        last = mm(o, xh[:, t % R2, :], w1_lo[:, ds(e, HID)], start=False, stop=True)
                    last.then_inc(Q["L1"], 1)
                if t - 2 in span:
                    u = t - 2
                    if u >= 2:
                        tile_after(pe, "hT", u - 2)
                    tile_after(pe, "hg", u)
                    for c in range(2 * KC):
                        last = nc.tensor.transpose(bank[4 + u % 2][:, c * P:(c + 1) * P], hg[:, u % R2, c * P:(c + 1) * P], ident[:, :])
                    last.then_inc(Q["Tg"], 1)
                if t - 3 in span:
                    u = t - 3
                    if u >= 2:
                        tile_after(pe, "ro", u - 2)
                    tile_after(pe, "hT", u)
                    for j, e in enumerate(offsets[u]):
                        for c in range(KC):
                            last = mm(bank[6 + u % 2][:, j * D:(j + 1) * D], hT[:, u % R2, j * KC + c, :],
                                      w2f[:, ds(e + c * D, D)], start=(c == 0), stop=(c == KC - 1))
                    last.then_inc(Q["L2"], 1)

            def walk(span):
                for t in steps(span):
                    step2(t, span)

            tiles(pe, walk)

        @block.scalar
        def _(act):
            fn = nc.scalar.activation

            for g in range(G):
                act.dma_start(blin[:, g, :], b_lin.unsqueeze(0)).then_inc(s_par, 16)
            act.wait_ge(s_early, 1)
            fn(warm[:, :], ones_f[0:1, 0:1], ACT.Sigmoid)
            act.wait_ge(s_const, 1)

            def edges_T(j):
                b = j % 2
                after(act, "YTp", j - 2)
                after(act, "Ep", j)
                for g in range(G):
                    last = fn(adjhT[:, b, g, :, :], pE[g][:, :].rearrange("p (h n) -> p h n", h=H), ACT.Copy)
                last.then_inc(S["adjhT"], 1)

            def attention(j):
                b = j % 2
                after(act, "adjh", j - 2)
                after(act, "S", j)
                for g in range(G):
                    last = fn(att[:, b, g, :, :], pS[g][:, :].rearrange("p (h n) -> p h n", h=H), ACT.Sigmoid, scale=SCALE)
                last.then_inc(S["att"], 1)

            def residual_norm(j):
                b = j % 2
                after(act, "n3Tp", j - 2)
                after(act, "rs3", j)
                after(act, "sh3", j)
                for g in range(G):
                    r = rows[:, j % RR, g, :]
                    last = fn(n3[:, b, g, :], r[:, 0:D], ACT.Identity, bias=r[:, C_SHIFT:C_SHIFT + 1], scale=r[:, C_RSTD:C_RSTD + 1])
                last.then_inc(S["n3"], 1)

            def exp_parts(j):
                b = j % 2
                after(act, "ez", j - 2)
                after(act, "zz", j)
                fn(sp[:, b, :, :], zz[:, b, :, :], ACT.Sigmoid).then_inc(S["sp"], 1)
                fn(sn[:, b, :, :], zz[:, b, :, :], ACT.Sigmoid, scale=-1.0).then_inc(S["sn"], 1)

            def project_out(j):
                b = j % 2
                after(act, "kl", j - 2)
                after(act, "qk", j)
                fn(qkc[:, b, :, :, :].rearrange("p a g n -> p (a g n)"), pQK[:, :], ACT.Copy).then_inc(S["qkc"], 1)

            def x_out(j):
                after(act, "xl", j - 2)
                after(act, "Xp", j)
                fn(xc[:, j % 2, :, :], pX[:, 0:GD].rearrange("p (g d) -> p g d", g=G), ACT.Copy).then_inc(S["xc"], 1)

            def norm(j):
                b = j % 2
                after(act, "nTp", j - 2)
                after(act, "rs1", j)
                after(act, "sh1", j)
                for g in range(G):
                    last = fn(nrm[:, b, g, :], xin[:, j % XR, g, :], ACT.Identity, bias=sh1[:, b, g:g + 1], scale=rs1[:, b, g:g + 1])
                last.then_inc(S["nrm"], 1)

            def aggregate_out(j):
                b = j % 2
                after(act, "Yp", j - 2)
                after(act, "YTp", j)
                fn(yT[:, b, :, :], pYT[:, 0:GD].rearrange("p (g n) -> p g n", g=G), ACT.Copy).then_inc(S["yT"], 1)

            def residual_T(j):
                b = j % 2
                after(act, "Lp", j - 2)
                after(act, "n3Tp", j)
                fn(n3T[:, b, :, :], pX[:, 0:GD].rearrange("p (g n) -> p g n", g=G), ACT.Copy).then_inc(S["n3T"], 1)

            def heads_apart(j):
                b = j % 2
                after(act, "S", j - 2)
                after(act, "ql", j)
                for h in range(H):
                    rng = slice(h * HD, (h + 1) * HD)
                    fn(qbd[rng, b, :, h, :], qkl[rng, b, 0, :, :], ACT.Copy).then_inc(S[f"qbd{h}"], 1)

            def norm_T(j):
                b = j % 2
                after(act, "Xp", j - 2)
                after(act, "nTp", j)
                fn(nrmT[:, b, :, :], pQK[:, 0:GD].rearrange("p (g n) -> p g n", g=G), ACT.Copy).then_inc(S["nrmT"], 1)

            for i in range(STEPS):
                run(attention, i - ATT)
                run(project_out, i - PROJ)
                run(edges_T, i - AGG)
                run(heads_apart, i - PROJ)
                run(x_out, i - PROJ)
                run(exp_parts, i - PLACE)
                run(residual_norm, i - GATE)
                run(norm, i - NORM)
                run(aggregate_out, i - AGG)
                run(residual_T, i - GATE)
                run(norm_T, i - NORM)
            act.wait_ge(s_w1, 16 * 4)
            fn(w1_hi[:, :], w1_sb[:, :], ACT.Copy).then_inc(s_w1hi, 1)
            act.wait_ge(s_plan, 1)
            fill_regions(act, ACT_FILLS, s_pad_act)
            fn(warm[:, :], ones_f[0:1, 0:1], ACT.Gelu)

            def step2(t, span):
                if t + 3 in span:
                    u = t + 3
                    row = rin[:, u % RIN, :]
                    if u >= R2:
                        tile_after(act, "T1", u - R2)
                    act.wait_ge(q_in[u % RIN], arrived(u, RIN))
                    fn(nx[:, u % R2, :], row[:, 0:D], ACT.Identity, bias=row[:, C_SHIFT:C_SHIFT + 1],
                       scale=row[:, C_RSTD:C_RSTD + 1]).then_inc(Q["nx"], 1)
                if t - 1 in span:
                    u = t - 1
                    if u >= R2:
                        tile_after(act, "Tg", u - R2)
                    tile_after(act, "hb", u)
                    fn(hg[:, u % R2, :], hb[:, u % R2, :], ACT.Gelu).then_inc(Q["hg"], 1)
                if t + 2 in span:
                    u = t + 2
                    if u >= R2:
                        tile_after(act, "L1", u - R2)
                    tile_after(act, "T1", u)
                    fn(xh[:, u % R2, :], bank[u % 2][:, 0:P], ACT.Copy).then_inc(Q["xh"], 1)
                if t - 2 in span:
                    u = t - 2
                    if u >= R2:
                        tile_after(act, "L2", u - R2)
                    tile_after(act, "Tg", u)
                    fn(hT[:, u % R2, :, :], bank[4 + u % 2][:, :].rearrange("p (c n) -> p c n", c=2 * KC), ACT.Copy).then_inc(Q["hT"], 1)

            def walk(span):
                for t in steps(span):
                    step2(t, span)

            tiles(act, walk)

        @block.gpsimd
        def _(pool):
            gp = nc.gpsimd
            gp.memset(ident[:, :], 0.0)
            gp.memset(neg_half[:, :], -0.5)
            gp.memset(eps_t[:, :], EPS)
            gp.memset(ones_f[:, :], 1.0)
            gp.memset(zero28[:, :], 0.0).then_inc(s_iota_c, 1)
            pool.wait_ge(s_iota_c, 1)
            gp.affine_select(out=ident[:, :], in_=ident[:, :], compare_op=ALU.not_equal, fill=1.0, base=0,
                             pattern=[[-1, P]], channel_multiplier=1).then_inc(s_early, 1)

            def later_constants():
                gp.memset(before[:, :], 1.0)
                gp.memset(ones[:, :], 1.0)
                gp.memset(b2_bc[:, :], 0.0).then_inc(s_bz, 1)
                gp.memset(filler[:, :], 0.0)
                gp.memset(rows[:, :, :, D:ROW], 0.0)
                gp.memset(seen[:, 0, :], 0.0).then_inc(s_iota_c, 1)
                pool.wait_ge(s_iota_c, 2)
                gp.affine_select(out=before[:, :], in_=before[:, :], compare_op=ALU.is_gt, fill=0.0, base=0,
                                 pattern=[[1, P]], channel_multiplier=-1)
                gp.iota(pair_no[:, :], [[1, NP]], base=0, channel_multiplier=0, allow_small_or_imprecise_dtypes=True)
                gp.iota(node_no[:, :], [[N, GRAPHS]], base=0, channel_multiplier=1)
                gp.iota(part_no[:, :], [[1, 1]], base=0, channel_multiplier=1, allow_small_or_imprecise_dtypes=True)
                for b in range(1, E):
                    gp.memset(tri[:, b - 1:b], float(b * (b - 1) // 2))
                gp.memset(filler[:, C_NODE:C_NODE + 1].bitcast(i32), NO_NODE).then_inc(s_iota, 1)

            def rstd(j, variance, vtmp, dst, has_var, has_vtmp, has_rstd, mean=None, less_mean=None):
                after(pool, has_var, j)
                gp.tensor_tensor(vtmp, variance, eps_t[:, :], ALU.add).then_inc(S[has_vtmp], 1)
                if mean is not None:
                    gp.tensor_tensor(less_mean, zero28[:, 0:G], mean, ALU.subtract)
                after(pool, has_vtmp, j)
                gp.tensor_tensor(dst, vtmp, neg_half[:, 0:G], ALU.pow).then_inc(S[has_rstd], 1)

            def scatter(j):
                r = j % RR
                after(pool, "slot", j)
                after(pool, "wa", j)
                after(pool, "node", j)
                for g in range(G):
                    gp.indirect_dma_start(
                        out=slots, out_offset=bass.IndirectOffsetOnAxis(ap=slot[:, j % 4, g:g + 1], axis=0),
                        in_=rows[:, r, g, :], in_offset=None, bounds_check=DUMMY_ROW + P - 1, oob_is_err=True,
                    ).then_inc(s_scat[r], 16)

            def shift(j, out, less_mean, rs, has_rstd, has_shift):
                after(pool, has_rstd, j)
                gp.tensor_tensor(out, less_mean, rs, ALU.mult).then_inc(S[has_shift], 1)

            def norm_rstd(j):
                b = j % 2
                after(pool, "nrm", j - 2)
                rstd(j, mv1[:, b, :, 1], ve1[:, b, :], rs1[:, b, :], "mv1", "ve1", "rs1", mv1[:, b, :, 0], lm1[:, b, :])
                shift(j, sh1[:, b, :], lm1[:, b, :], rs1[:, b, :], "rs1", "sh1")

            def aggregate_rstd(j):
                b = j % 2
                after(pool, "res", j - 2)
                rstd(j, mv2[:, b, :, 1], ve2[:, b, :], rs2[:, b, :], "mv2", "ve2", "rs2")

            def residual_rstd(j):
                b, r = j % 2, j % RR
                after(pool, "n3", j - 2)
                rstd(j, rows[:, r, :, C_VAR], ve3[:, b, :], rows[:, r, :, C_RSTD], "mv3", "ve3", "rs3",
                     rows[:, r, :, C_MEAN], lm3[:, b, :])
                shift(j, rows[:, r, :, C_SHIFT], lm3[:, b, :], rows[:, r, :, C_RSTD], "rs3", "sh3")
                gp.tensor_copy(rows[:, r, :, C_NODE].bitcast(i32), node_no[:, j * G:(j + 1) * G]).then_inc(S["node"], 1)

            def degrees(j):
                b = j % 2
                after(pool, "degc", j)
                after(pool, "degm", j)
                gp.tensor_tensor(degp[:, b, :], degc[:, b, :], neg_half[:, :], ALU.pow).then_inc(S["degp"], 1)
                after(pool, "degp", j)
                after(pool, "yv", j - 4)
                gp.tensor_tensor(dis[:, j % 4, :], degp[:, b, :], degm[:, b, :], ALU.mult).then_inc(S["dis"], 1)

            def weights(j):
                b, r = j % 2, j % RR
                after(pool, "w12", j)
                after(pool, "sel", j)
                gp.tensor_tensor(dw[:, b, :], w12[:, b, :, 0], w12[:, b, :, 1], ALU.subtract).then_inc(S["dw"], 1)
                after(pool, "dw", j)
                gp.tensor_tensor(sdw[:, b, :], dw[:, b, :], sel[:, b, :], ALU.mult).then_inc(S["sdw"], 1)
                after(pool, "sdw", j)
                gp.tensor_tensor(rows[:, r, :, C_WA], w12[:, b, :, 1], sdw[:, b, :], ALU.add)
                gp.tensor_tensor(rows[:, r, :, C_WB], w12[:, b, :, 0], sdw[:, b, :], ALU.subtract).then_inc(S["wa"], 1)

            for i in range(STEPS):
                run(norm_rstd, i - NORM)
                if i == 0:
                    later_constants()
                run(aggregate_rstd, i - RES)
                run(scatter, i - SCAT)
                run(degrees, i - ATT)
                run(residual_rstd, i - RES)
                run(weights, i - PLACE)

            pool.wait_ge(s_plan, 1)
            fill_regions(pool, POOL_FILLS, s_pad_pool)

            def store(span):
                for u in span:
                    tile_after(pool, "ro", u)
                    gp.indirect_dma_start(
                        out=out_rows, out_offset=bass.IndirectOffsetOnAxis(ap=rin[:, u % RIN, C_NODE:C_NODE + 1].bitcast(u32), axis=0),
                        in_=ro[:, u % RO, :], in_offset=None, bounds_check=NODES - 1, oob_is_err=False,
                    ).then_inc(q_out[u % RO], 16)
                for r in range(RO):
                    pool.wait_ge(q_out[r], 16 * len(range(r, span.stop, RO)))

            pool.wait_ge(s_desc, 1)
            tiles(pool, store)

        @block.vector
        def _(dve):
            v = nc.vector

            for b in range(2):
                last = v.memset(qbd[:, b, :, :, :], 0.0)
            last.then_inc(s_const, 1)

            def flat(t):
                return t.rearrange("p g d -> p (g d)")

            def by_head(t):
                return t.rearrange("p g (h d) -> p (g h) d", h=H)

            def over_graphs(t):
                return t.unsqueeze(1).to_broadcast([P, G, D])

            def norm_stats(j):
                dve.wait_ge(s_x[j % XR], arrived(j, XR))
                for g in range(G):
                    last = v.bn_stats(st1[:, j % 2, g, :], xin[:, j % XR, g, :])
                last.then_inc(S["st1"], 1)

            def norm_mean_var(j):
                after(dve, "st1", j)
                after(dve, "sh1", j - 2)
                for g in range(G):
                    last = v.bn_aggr(mv1[:, j % 2, g, :], st1[:, j % 2, g, :])
                last.then_inc(S["mv1"], 1)

            def pair_of_experts_1(j):
                b = j % 2
                after(dve, "eb", j)
                v.scalar_tensor_tensor(tb[:, b, :], eb[:, b, :], -1.0, eb[:, b, :], ALU.add, ALU.mult).then_inc(S["tb"], 1)

            def pair_of_experts_2(j):
                b = j % 2
                after(dve, "tb", j)
                after(dve, "ea", j)
                v.scalar_tensor_tensor(pid[:, b, :], tb[:, b, :], 0.5, ea[:, b, :], ALU.mult, ALU.add).then_inc(S["pid"], 1)

            def one_hot(j):
                b = j % 2
                after(dve, "rank", j - 2)
                after(dve, "pid", j)
                v.tensor_tensor(oh[:, b, :, :], pair_no[:, :].unsqueeze(1).to_broadcast([P, G, NP]),
                                pid[:, b, :].unsqueeze(2).to_broadcast([P, G, NP]), ALU.is_equal).then_inc(S["oh"], 1)

            def seen_1(j):
                b = j % 2
                after(dve, "oh", j)
                after(dve, "seen", j - 1)
                v.tensor_tensor(seen1[:, b, :], seen[:, b, :], oh[:, b, 0, :], ALU.add).then_inc(S["seen1"], 1)

            def seen_2(j):
                b = j % 2
                after(dve, "rank", j - 1)
                after(dve, "seen1", j)
                v.tensor_tensor(seen[:, 1 - b, :], seen1[:, b, :], oh[:, b, 1, :], ALU.add).then_inc(S["seen"], 1)

            def scale_x(j):
                b = j % 2
                after(dve, "dis", j)
                after(dve, "xl", j)
                after(dve, "YTp", j - 2)
                v.tensor_tensor(by_head(xs[:, b, :, :]), by_head(xl[:, j % 4, :, :]),
                                dis[:, j % 4, :].unsqueeze(2).to_broadcast([P, GH, HD]), ALU.mult).then_inc(S["xs"], 1)

            def scale_y(j):
                b = j % 2
                after(dve, "Yp", j)
                after(dve, "dis", j)
                v.tensor_tensor(by_head(yv[:, b, :, :]), pY[:, 0:GD].rearrange("p (c d) -> p c d", d=HD),
                                dis[:, j % 4, :].unsqueeze(2).to_broadcast([P, GH, HD]), ALU.mult).then_inc(S["yv"], 1)

            def leaky_x(j):
                after(dve, "xc", j)
                z = flat(xc[:, j % 2, :, :])
                v.scalar_tensor_tensor(flat(xl[:, j % 4, :, :]), z, LEAK, z, ALU.mult, ALU.max).then_inc(S["xl"], 1)

            def leaky_qk(j):
                b = j % 2
                after(dve, "S", j - 2)
                after(dve, "qkc", j)
                for a, name in enumerate(("ql", "kl")):
                    z = flat(qkc[:, b, a, :, :])
                    v.scalar_tensor_tensor(flat(qkl[:, b, a, :, :]), z, LEAK, z, ALU.mult, ALU.max).then_inc(S[name], 1)

            def aggregate_stats(j):
                b = j % 2
                after(dve, "yv", j)
                for g in range(G):
                    last = v.bn_stats(st2[:, b, g, :], yv[:, b, g, :])
                last.then_inc(S["st2"], 1)

            def aggregate_mean_var(j):
                b = j % 2
                after(dve, "st2", j)
                for g in range(G):
                    last = v.bn_aggr(mv2[:, b, g, :], st2[:, b, g, :])
                last.then_inc(S["mv2"], 1)

            def x_plus_b(j):
                if j == 0:
                    dve.wait_ge(s_par2, 16 * 5)
                v.tensor_tensor(xb[:, j % 2, :, :], xin[:, j % XR, :, :], over_graphs(lnb_bc[:, :]), ALU.add).then_inc(S["xb"], 1)

            def edges(j, g):
                b = j % 2
                if g == 0:
                    after(dve, "att", j)
                    after(dve, "Ep", j - 2)
                    dve.wait_ge(s_adj[j % AR], arrived(j, AR))
                for h in range(H):
                    c = g * H + h
                    last = v.scalar_tensor_tensor(adjh[:, b, g, h, :], att[:, b, g, h, :], 1.0, adjin[:, j % AR, g, :],
                                                  ALU.mult, ALU.mult, accum_out=deg[:, b, c:c + 1])
                if g == G - 1:
                    last.then_inc(S["adjh"], 1)

            def edges_0(j):
                edges(j, 0)

            def edges_1(j):
                edges(j, 1)

            def degrees(j):
                b = j % 2
                after(dve, "adjh", j)
                after(dve, "dis", j - 2)
                v.tensor_scalar(degc[:, b, :], deg[:, b, :], TINY, None, ALU.max).then_inc(S["degc"], 1)
                v.tensor_scalar(degm[:, b, :], deg[:, b, :], 0.0, None, ALU.is_gt).then_inc(S["degm"], 1)

            def aggregate_gain(j):
                b = j % 2
                after(dve, "mv2", j)
                for g in range(G):
                    last = v.scalar_tensor_tensor(yg[:, b, g, :], yv[:, b, g, :], mv2[:, b, g, 0:1], lng_bc[:, :],
                                                  ALU.subtract, ALU.mult)
                last.then_inc(S["yg"], 1)

            def residual(j):
                b, r = j % 2, j % RR
                if j == 0:
                    dve.wait_ge(s_iota, 1)
                after(dve, "yg", j)
                after(dve, "xb", j)
                after(dve, "rs2", j)
                if j >= RR:
                    dve.wait_ge(s_scat[r], arrived(j - RR, RR, 16 * G))
                for g in range(G):
                    last = v.scalar_tensor_tensor(rows[:, r, g, 0:D], yg[:, b, g, :], rs2[:, b, g:g + 1], xb[:, b, g, :],
                                                  ALU.mult, ALU.add)
                last.then_inc(S["res"], 1)

            def residual_stats(j):
                after(dve, "res", j)
                for g in range(G):
                    last = v.bn_stats(st3[:, j % 2, g, :], rows[:, j % RR, g, 0:D])
                last.then_inc(S["st3"], 1)

            def residual_mean_var(j):
                after(dve, "st3", j)
                for g in range(G):
                    last = v.bn_aggr(rows[:, j % RR, g, C_MEAN:C_MEAN + 2], st3[:, j % 2, g, :])
                last.then_inc(S["mv3"], 1)

            def top(j):
                after(dve, "Lp", j)
                for g in range(G):
                    last = v.max(mx[:, j % 2, g, :], pYT[:, g * E:(g + 1) * E])
                last.then_inc(S["mx"], 1)

            def top_index(j):
                after(dve, "mx", j)
                for g in range(G):
                    last = v.max_index(ix[:, j % 2, g, :], mx[:, j % 2, g, :], pYT[:, g * E:(g + 1) * E])
                last.then_inc(S["ix"], 1)

            def less_max(j):
                b = j % 2
                after(dve, "sn", j - 2)
                v.tensor_tensor(zz[:, b, :, :], mx[:, b, :, :], mx[:, b, :, 0:1].to_broadcast([P, G, E]),
                                ALU.subtract).then_inc(S["zz"], 1)

            def order_experts(j):
                b = j % 2
                after(dve, "ix", j)
                after(dve, "sdw", j - 2)
                v.tensor_tensor(eb[:, b, :], ix[:, b, :, 0], ix[:, b, :, 1], ALU.max).then_inc(S["eb"], 1)
                v.tensor_tensor(ea[:, b, :], ix[:, b, :, 0], ix[:, b, :, 1], ALU.min).then_inc(S["ea"], 1)
                v.tensor_tensor(sel[:, b, :], ix[:, b, :, 0], ix[:, b, :, 1], ALU.is_lt).then_inc(S["sel"], 1)

            def exp_1(j):
                after(dve, "sn", j)
                v.reciprocal(rn[:, j % 2, :, :], sn[:, j % 2, :, :]).then_inc(S["rn"], 1)

            def exp_2(j):
                b = j % 2
                after(dve, "sp", j)
                after(dve, "rn", j)
                v.tensor_tensor(ez[:, b, :, :], sp[:, b, :, :], rn[:, b, :, :], ALU.mult).then_inc(S["ez"], 1)

            def exp_sum(j):
                after(dve, "ez", j)
                v.tensor_reduce(es[:, j % 2, :], ez[:, j % 2, :, :], AX.X, ALU.add).then_inc(S["es"], 1)

            def exp_sum_inverse(j):
                after(dve, "es", j)
                v.reciprocal(er[:, j % 2, :], es[:, j % 2, :]).then_inc(S["er"], 1)

            def weights(j):
                b = j % 2
                after(dve, "er", j)
                after(dve, "wa", j - 2)
                v.tensor_tensor(w12[:, b, :, :], ez[:, b, :, 0:2], er[:, b, :].unsqueeze(2).to_broadcast([P, G, 2]),
                                ALU.mult).then_inc(S["w12"], 1)

            def position(j):
                b = j % 2
                after(dve, "rank", j)
                for g in range(G):
                    last = v.scalar_tensor_tensor(own[:, g, :], oh[:, b, g, :], 1.0, pY[:, GD + g * NP:GD + (g + 1) * NP],
                                                  ALU.mult, ALU.mult, accum_out=pos[:, b, g:g + 1])
                last.then_inc(S["pos"], 1)

            def to_slot(j):
                b = j % 2
                if j >= 4:
                    dve.wait_ge(s_scat[(j - 4) % RR], arrived(j - 4, RR, 16 * G))
                after(dve, "pos", j)
                v.scalar_tensor_tensor(slot[:, j % 4, :], pid[:, b, :], float(REGION), pos[:, b, :],
                                       ALU.mult, ALU.add).then_inc(S["slot"], 1)

            for i in range(STEPS):
                run(pair_of_experts_1, i - PLACE)
                run(norm_stats, i - NORM)
                run(pair_of_experts_2, i - PLACE)
                run(scale_x, i - AGG)
                run(norm_mean_var, i - NORM)
                run(one_hot, i - PLACE)
                run(scale_y, i - RES)
                run(seen_1, i - PLACE)
                run(aggregate_stats, i - RES)
                run(leaky_qk, i - PROJ)
                run(aggregate_mean_var, i - RES)
                run(edges_0, i - ATT)
                run(seen_2, i - PLACE)
                run(edges_1, i - ATT)
                run(x_plus_b, i - RES)
                run(position, i - PLACE)
                run(exp_1, i - PLACE)
                run(aggregate_gain, i - RES)
                run(degrees, i - ATT)
                run(exp_2, i - PLACE)
                run(leaky_x, i - PROJ)
                run(residual, i - RES)
                run(to_slot, i - PLACE)
                run(exp_sum, i - PLACE)
                run(residual_stats, i - RES)
                run(exp_sum_inverse, i - PLACE)
                run(top, i - GATE)
                run(residual_mean_var, i - RES)
                run(top_index, i - GATE)
                run(weights, i - PLACE)
                run(less_max, i - GATE)
                run(order_experts, i - GATE)
            n_plan = [0]

            def then(ins):
                n_plan[0] += 1
                ins.then_inc(s_chain, 1)
                dve.wait_ge(s_chain, n_plan[0])

            dve.wait_ge(s_cnt, 1)
            then(v.tensor_copy(cnt[:, :], bank[7][:, 0:NP]))
            then(v.tensor_scalar(cnti[:, :], cnt[:, :], float(P - 1), None, ALU.add))
            v.scalar_tensor_tensor(padrow[:, :], pair_no[:, :], float(REGION), cnt[:, :], ALU.mult, ALU.add).then_inc(s_plan, 1)
            then(v.tensor_scalar(tilesi[:, :], cnti[:, :], P.bit_length() - 1, None, ALU.logical_shift_right))
            then(v.tensor_copy(tilesf[:, :], tilesi[:, :]))
            then(v.tensor_tensor_scan(cum[:, :], tilesf[:, :], zero28[:, :], 0.0, ALU.add, ALU.add))
            then(v.tensor_copy(tiles_used[:, :], cum[:, NP - 1:NP]))
            then(v.tensor_scalar(past[:, :], cum[:, :], part_no[:, 0:1], None, ALU.is_le))
            then(v.reduce_sum(tinfo[:, 3:4], past[:, :], AX.X))
            then(v.scalar_tensor_tensor(scr28[:, :], past[:, :], 1.0, tilesf[:, :], ALU.mult, ALU.mult, accum_out=tinfo[:, 4:5]))
            then(v.tensor_tensor(tinfo[:, 5:6], part_no[:, :], tinfo[:, 4:5], ALU.subtract))
            then(v.tensor_scalar(tinfo[:, 6:7], tinfo[:, 5:6], float(P), None, ALU.mult))
            then(v.scalar_tensor_tensor(tinfo[:, 7:8], tinfo[:, 3:4], float(REGION), tinfo[:, 6:7], ALU.mult, ALU.add))
            then(v.tensor_scalar(tinfo[:, 0:1], tinfo[:, 7:8], float(DUMMY_ROW), None, ALU.min))
            then(v.tensor_scalar(ge7[:, :], tri[:, :], tinfo[:, 3:4], None, ALU.is_le))
            then(v.reduce_sum(tinfo[:, 2:3], ge7[:, :], AX.X))
            then(v.scalar_tensor_tensor(tinfo[:, 4:5], tinfo[:, 2:3], -1.0, tinfo[:, 2:3], ALU.add, ALU.mult))
            then(v.scalar_tensor_tensor(tinfo[:, 1:2], tinfo[:, 4:5], -0.5, tinfo[:, 3:4], ALU.mult, ALU.add))
            then(v.tensor_scalar(tinfo[:, 2:3], tinfo[:, 2:3], float(PACK * HID), None, ALU.mult))
            v.scalar_tensor_tensor(tinfo[:, 1:2], tinfo[:, 1:2], float(HID), tinfo[:, 2:3], ALU.mult, ALU.add).then_inc(s_tin, 1)
            dve.wait_ge(s_descp, 1)
            v.tensor_copy(desc[0:1, :], bank[7][0:1, 128:128 + 3 * P]).then_inc(s_desc, 1)
            dve.wait_ge(s_desc, 1)

            dve.wait_ge(s_w1hi, 1)
            v.tensor_tensor(w1_lo[:, :], w1_sb[:, :], w1_hi[:, :].bitcast(f32), ALU.subtract).then_inc(s_w1lo, 1)

            experts = {}

            def add_b2(u, j, dst, prior, name):
                v.scalar_tensor_tensor(dst[:, u % R2, :], b2_bc[:, ds(experts[u][j], D)], rin[:, u % RIN, C_WA + j:C_WA + j + 1],
                                       prior, ALU.mult, ALU.add).then_inc(Q[name], 1)

            def add_y(u, j, dst, prior, name):
                v.scalar_tensor_tensor(dst, bank[6 + u % 2][:, j * D:(j + 1) * D], rin[:, u % RIN, C_WA + j:C_WA + j + 1],
                                       prior, ALU.mult, ALU.add).then_inc(Q[name], 1)

            def step2(t, span):
                u = t - 4
                if t in span:
                    if t == span.start:
                        experts[t] = expert_offsets(dve, t)
                    if t >= R2:
                        tile_after(dve, "hg", t - R2)
                    tile_after(dve, "L1", t)
                    for j, e in enumerate(experts[t]):
                        last = v.tensor_tensor(hb[:, t % R2, j * HID:(j + 1) * HID], bank[2 + t % 2][:, j * HID:(j + 1) * HID],
                                               b1_bc[:, ds(e, HID)], ALU.add)
                    last.then_inc(Q["hb"], 1)
                if u in span:
                    tile_after(dve, "rb", u)
                    tile_after(dve, "L2", u)
                    add_y(u, 0, rc[:, u % R2, :], rb[:, u % R2, :], "rc")
                if u + 1 in span:
                    dve.wait_ge(q_in[(u + 1) % RIN], arrived(u + 1, RIN))
                    add_b2(u + 1, 0, ra, rin[:, (u + 1) % RIN, 0:D], "ra")
                if t + 1 in span and t in span:
                    experts[t + 1] = expert_offsets(dve, t + 1)
                if u in span:
                    if u >= RO:
                        dve.wait_ge(q_out[u % RO], arrived(u - RO, RO))
                    tile_after(dve, "rc", u)
                    add_y(u, 1, ro[:, u % RO, :], rc[:, u % R2, :], "ro")
                if u + 1 in span:
                    tile_after(dve, "ra", u + 1)
                    add_b2(u + 1, 1, rb, ra[:, (u + 1) % R2, :], "rb")
                if t + 2 in span:
                    u = t + 2
                    if u >= R2:
                        tile_after(dve, "L1", u - R2)
                    tile_after(dve, "xh", u)
                    v.tensor_tensor(xo[:, u % R2, :], bank[u % 2][:, 0:P], xh[:, u % R2, :].bitcast(f32), ALU.subtract).then_inc(Q["xo"], 1)

            def walk(span):
                for t in steps(span):
                    step2(t, span)

            tiles(dve, walk)


_INS = ['x', 'adj', 'L0_gnn_W_lin', 'L0_gnn_b_lin', 'L0_gnn_W_q', 'L0_gnn_W_k', 'L0_gnn_ln_g', 'L0_gnn_ln_b',
        'L0_ffn_gate_w', 'L0_ffn_gate_b', 'L0_ffn_W1', 'L0_ffn_b1', 'L0_ffn_W2', 'L0_ffn_b2']
_OUTS = [((64, 128, 128), 'float32')]


def kernel(**inputs):
    import numpy as _np
    import concourse.bacc as _bacc
    from concourse import mybir as _mybir
    from concourse.bass_utils import run_bass_kernel_spmd as _run

    nc = _bacc.Bacc("TRN2", target_bir_lowering=False, num_devices=1)
    arrays, args = {}, []
    for name in _INS:
        a = _np.ascontiguousarray(inputs[name])
        arrays[f"in_{name}_dram"] = a
        args.append(nc.dram_tensor(f"in_{name}_dram", a.shape, _mybir.dt.from_np(a.dtype), kind="ExternalInput").ap())
    for i, (shape, dtype) in enumerate(_OUTS):
        dt = _mybir.dt.from_np(_np.dtype(dtype))
        args.append(nc.dram_tensor(f"out_{i}_dram", shape, dt, kind="ExternalOutput").ap())
    graph_block_kernel(nc, *args)
    r = _run(nc, [arrays], core_ids=[0])
    return r.results[0]["out_0_dram"]
```
